# Optimizing a Trainium2 kernel written in Bass

```python
import numpy as np
import jax
import jax.numpy as jnp

def _softmax(x, axis=-1):
    return jax.nn.softmax(x, axis=axis)

def _gelu(x):
    return jax.nn.gelu(x, approximate=True)

def _silu(x):
    return jax.nn.silu(x)

def _sigmoid(x):
    return jax.nn.sigmoid(x)

def _layernorm(x, axis=-1, eps=1e-05):
    m = jnp.mean(x, axis=axis, keepdims=True)
    v = jnp.var(x, axis=axis, keepdims=True)
    return (x - m) / jnp.sqrt(v + eps)

def _scatter_add(tgt, idx, src, axis=0):
    return tgt.at[idx].add(src)

def _segment_sum(src, seg, n):
    return jax.ops.segment_sum(src, seg, n)
kernel_name = 'mk_gps_d1_gnn_r32_d892ab'

def setup_inputs(seed: int=0):
    np.random.seed(seed)
    _w = jnp.asarray

    def _rec_inputs():
        import jax
        import jax.numpy as jnp
        _gk = jax.random.key(seed)
        x = -0.0003713 + 1 * jax.random.normal(jax.random.fold_in(_gk, 1), (3125, 256), jnp.float32)
        src = jax.random.randint(jax.random.fold_in(_gk, 2), (50000,), 0, 3125, jnp.int32)
        dst = jnp.minimum((3125 * jax.random.uniform(jax.random.fold_in(_gk, 3), (50000,)) ** 2.0).astype(jnp.int32), 99999)
        _o = jnp.argsort(dst, stable=True)
        src = src[_o]
        dst = dst[_o]
        edge_weight = jax.random.uniform(jax.random.fold_in(_gk, 12), (50000,), jnp.float32, 0.0, 0.999998)
        return (x, src, dst, edge_weight)
    x, src, dst, edge_weight = _rec_inputs()

    def _L0_gnn_setup():
        import jax, jax.numpy as jnp
        import numpy as np
        N_NODES = 50000
        N_EDGES = 25000
        IN_F = 256
        OUT_F = 64
        HEADS = 4
        NEG_SLOPE = 0.2
        key = jax.random.key(seed)
        ks = jax.random.split(key, 6)
        x = jax.random.normal(ks[0], (N_NODES, IN_F), dtype=jnp.float32)
        edge_index = jax.random.randint(ks[1], (2, N_EDGES), 0, N_NODES, dtype=jnp.int32)
        edge_weight = jax.random.uniform(ks[2], (N_EDGES,), dtype=jnp.float32)
        gain = float(np.sqrt(2.0 / (1.0 + NEG_SLOPE ** 2)))
        w_bound = gain * np.sqrt(6.0 / (IN_F + OUT_F))
        a_bound = gain * np.sqrt(6.0 / (OUT_F + 1))
        W = jax.random.uniform(ks[3], (HEADS, IN_F, OUT_F), minval=-w_bound, maxval=w_bound, dtype=jnp.float32)
        a_src = jax.random.uniform(ks[4], (HEADS, OUT_F, 1), minval=-a_bound, maxval=a_bound, dtype=jnp.float32)
        a_dst = jax.random.uniform(ks[5], (HEADS, OUT_F, 1), minval=-a_bound, maxval=a_bound, dtype=jnp.float32)
        return {'x': x, 'edge_index': edge_index, 'edge_weight': edge_weight, 'W': W, 'a_src': a_src, 'a_dst': a_dst}
    _L0_gnn_all = _L0_gnn_setup()
    _L0_gnn_in = {k: v for k, v in _L0_gnn_all.items() if k in ('W', 'a_src', 'a_dst')}
    del _L0_gnn_all

    def _L0_mix_setup():
        import jax, jax.numpy as jnp
        import numpy as np
        HEADS = 4
        DIM_HEAD = 32
        key = jax.random.key(seed)
        k1, k2, k3 = jax.random.split(key, 3)
        B, L, D = (16, 256, 256)
        hidden = HEADS * DIM_HEAD
        x = jax.random.normal(k1, (B, L, D), dtype=jnp.float32)
        W_qkv = jax.random.normal(k2, (D, 3 * hidden), dtype=jnp.float32) * D ** (-0.5)
        W_out = jax.random.normal(k3, (hidden, D), dtype=jnp.float32) * hidden ** (-0.5)
        b_out = jnp.zeros((D,), dtype=jnp.float32)
        return {'x': x, 'W_qkv': W_qkv, 'W_out': W_out, 'b_out': b_out}
    _L0_mix_all = _L0_mix_setup()
    _L0_mix_in = {k: v for k, v in _L0_mix_all.items() if k in ('W_qkv', 'W_out', 'b_out')}
    del _L0_mix_all

    def _L0_ffn_setup():
        import jax, jax.numpy as jnp
        import numpy as np
        B, S, D = (8, 128, 256)
        H = 4 * D
        CAPACITY = 0.5
        key = jax.random.key(seed)
        ks = jax.random.split(key, 6)
        x = jax.random.normal(ks[0], (B, S, D), dtype=jnp.float32)
        attention_mask = jnp.zeros((B, 1, 1, S), dtype=jnp.float32)
        wr = jax.random.normal(ks[1], (D, 1), dtype=jnp.float32) * 0.02
        br = jnp.zeros((1,), dtype=jnp.float32)
        w1 = jax.random.normal(ks[2], (D, H), dtype=jnp.float32) * 0.02
        b1 = jnp.zeros((H,), dtype=jnp.float32)
        w2 = jax.random.normal(ks[3], (H, D), dtype=jnp.float32) * 0.02
        b2 = jnp.zeros((D,), dtype=jnp.float32)
        return {'x': x, 'attention_mask': attention_mask, 'wr': wr, 'br': br, 'w1': w1, 'b1': b1, 'w2': w2, 'b2': b2}
    _L0_ffn_all = _L0_ffn_setup()
    _L0_ffn_in = {k: v for k, v in _L0_ffn_all.items() if k in ('attention_mask', 'wr', 'br', 'w1', 'b1', 'w2', 'b2')}
    del _L0_ffn_all
    return {'x': x, 'src': src, 'dst': dst, 'edge_weight': edge_weight, 'L0_gnn_W': _L0_gnn_in['W'], 'L0_gnn_a_src': _L0_gnn_in['a_src'], 'L0_gnn_a_dst': _L0_gnn_in['a_dst'], 'L0_mix_W_qkv': _L0_mix_in['W_qkv'], 'L0_mix_W_out': _L0_mix_in['W_out'], 'L0_mix_b_out': _L0_mix_in['b_out'], 'L0_ffn_attention_mask': _L0_ffn_in['attention_mask'], 'L0_ffn_wr': _L0_ffn_in['wr'], 'L0_ffn_br': _L0_ffn_in['br'], 'L0_ffn_w1': _L0_ffn_in['w1'], 'L0_ffn_b1': _L0_ffn_in['b1'], 'L0_ffn_w2': _L0_ffn_in['w2'], 'L0_ffn_b2': _L0_ffn_in['b2']}

def reference(x, src, dst, edge_weight, L0_gnn_W, L0_gnn_a_src, L0_gnn_a_dst, L0_mix_W_qkv, L0_mix_W_out, L0_mix_b_out, L0_ffn_attention_mask, L0_ffn_wr, L0_ffn_br, L0_ffn_w1, L0_ffn_b1, L0_ffn_w2, L0_ffn_b2):
    import jax
    import jax.numpy as jnp

    def _L0_gnn_ref(x, edge_index, edge_weight, W, a_src, a_dst):
        import jax, jax.numpy as jnp
        import numpy as np
        N_NODES = 50000
        N_EDGES = 25000
        IN_F = 256
        OUT_F = 64
        HEADS = 4
        NEG_SLOPE = 0.2
        num_nodes = x.shape[0]
        h = jnp.einsum('ni,hio->hno', x, W)
        attn_src = jnp.einsum('hno,hod->hn', h, a_src)
        attn_dst = jnp.einsum('hno,hod->hn', h, a_dst)
        src_idx, dst_idx = (edge_index[0], edge_index[1])
        e = attn_src[:, src_idx] + attn_dst[:, dst_idx]
        e = jnp.where(e >= 0, e, NEG_SLOPE * e)
        e = e * edge_weight[None, :]
        e_exp = jnp.exp(e - jnp.max(e))
        denom = jax.ops.segment_sum(e_exp.T, dst_idx, num_segments=num_nodes).T
        alpha = e_exp / (denom[:, dst_idx] + 1e-10)
        msg = h[:, src_idx] * alpha[..., None]
        out = jax.vmap(lambda m: jax.ops.segment_sum(m, dst_idx, num_segments=num_nodes))(msg)
        return jnp.transpose(out, (1, 0, 2)).reshape(num_nodes, HEADS * OUT_F)

    def _L0_mix_ref(x, W_qkv, W_out, b_out):
        import jax, jax.numpy as jnp
        import numpy as np
        HEADS = 4
        DIM_HEAD = 32
        B, L, D = x.shape
        scale = DIM_HEAD ** (-0.5)
        qkv = jnp.einsum('bld,df->blf', x, W_qkv)
        qkv = qkv.reshape(B, L, 3, HEADS, DIM_HEAD)
        q = jnp.transpose(qkv[:, :, 0], (0, 2, 1, 3)) * scale
        k = jax.nn.softmax(jnp.transpose(qkv[:, :, 1], (0, 2, 1, 3)), axis=2)
        v = jnp.transpose(qkv[:, :, 2], (0, 2, 1, 3))
        context = jnp.einsum('bhld,bhle->bhde', k, v)
        out = jnp.einsum('bhde,bhld->bhle', context, q)
        out = jnp.transpose(out, (0, 2, 1, 3)).reshape(B, L, HEADS * DIM_HEAD)
        return jnp.einsum('blf,fd->bld', out, W_out) + b_out

    def _L0_ffn_ref(x, attention_mask, wr, br, w1, b1, w2, b2):
        import jax, jax.numpy as jnp
        import numpy as np
        B, S, D = (8, 128, 256)
        H = 4 * D
        CAPACITY = 0.5
        b, s, d = x.shape
        weights = (jnp.einsum('bsd,do->bso', x, wr) + br)[..., 0]
        k = max(1, int(CAPACITY * s))
        kk = k - 1 if k > 1 else 1
        _, idx = jax.lax.top_k(weights, k)
        sel_idx = idx[:, :kk]
        sel = jnp.take_along_axis(x, sel_idx[:, :, None], axis=1)
        h = jax.nn.gelu(jnp.einsum('bkd,dh->bkh', sel, w1) + b1)
        y = jnp.einsum('bkh,hd->bkd', h, w2) + b2
        w_sel = jnp.take_along_axis(weights, sel_idx, axis=1)
        y = y * w_sel[..., None]
        batch_idx = jnp.arange(b)[:, None]
        processed = jnp.zeros_like(x).at[batch_idx, sel_idx].set(y)
        return processed + x
    edge_index = jnp.stack([src, dst])
    xn = _layernorm(x, axis=-1)
    x = x + _L0_gnn_ref(xn, edge_index, edge_weight, L0_gnn_W, L0_gnn_a_src, L0_gnn_a_dst) + _L0_mix_ref(xn[None], L0_mix_W_qkv, L0_mix_W_out, L0_mix_b_out)[0]
    x = x + _L0_ffn_ref(_layernorm(x, axis=-1)[None], L0_ffn_attention_mask, L0_ffn_wr, L0_ffn_br, L0_ffn_w1, L0_ffn_b1, L0_ffn_w2, L0_ffn_b2)[0]
    return x

_drawn_inputs = setup_inputs


def setup_inputs(seed=0):
    import zlib

    import numpy as np

    out = dict(_drawn_inputs(seed))
    spreads = {'L0_mix_b_out': (0.0, 0.1), 'L0_ffn_b1': (0.0, 0.8), 'L0_ffn_b2': (0.0, 0.8)}
    factors = {'L0_ffn_wr': 5.06, 'L0_ffn_w1': 5.601, 'L0_ffn_w2': 5.263}
    for name, (base, spread) in spreads.items():
        noise = np.random.default_rng([zlib.crc32(name.encode()), seed]).standard_normal(out[name].shape)
        drawn = base * np.exp(spread * noise) if base else spread * noise
        out[name] = jnp.asarray(drawn.astype(out[name].dtype))
    for name, factor in factors.items():
        out[name] = (out[name] * factor).astype(out[name].dtype)
    return out
```

```python
from contextlib import ExitStack

import numpy as np
import concourse.bass as bass
from concourse import mybir

P = 128
F32 = mybir.dt.float32
BF16 = mybir.dt.bfloat16
I32 = mybir.dt.int32
U16 = mybir.dt.uint16
ALU = mybir.AluOpType
ACT = mybir.ActivationFunctionType
AX = mybir.AxisListType

HEADS, OUT_F = 4, 64
MIX_HEADS, DIM_HEAD = 4, 32
NEG_SLOPE, LN_EPS, DEN_EPS = 0.2, 1e-5, 1e-10
LOWEST = -3.0e38
TILES = 4
RING = 4
BODY = 5


def gps_layer(nc, x_in, src_in, dst_in, ew_in, gw_in, gas_in, gad_in, wqkv_in, wout_in, bout_in,
              wr_in, br_in, w1_in, b1_in, w2_in, b2_in, out):
    N, D = x_in.shape
    E = src_in.shape[0]
    NB = -(-N // P)
    REST = N - (NB - 1) * P
    HF = HEADS * OUT_F
    ROW = HF + HEADS
    QK = MIX_HEADS * DIM_HEAD
    ADV = HEADS + QK
    HW = ROW + ADV
    FF = w1_in.shape[1]
    FC = FF // P
    KC = D // P
    GE = TILES * P
    NG = -(-E // GE)
    EREST = E - (NG - 1) * GE
    PAD = GE - EREST
    PREST = EREST // TILES
    LOOPS = NG // RING
    KSEL = max(1, int(0.5 * N))
    KK = KSEL - 1 if KSEL > 1 else 1
    assert EREST % TILES == 0 and D == HF == 256 and NB % BODY == 0 and QK == P

    htab = nc.dram_tensor("htab", (NB * P, ROW), F32, kind="Internal").ap()
    dstu_d = nc.dram_tensor("dstu_d", (NG, GE), U16, kind="Internal").ap()
    meta_d = nc.dram_tensor("meta_d", (NG, 2), I32, kind="Internal").ap()
    w_d = nc.dram_tensor("w_d", (NB, P), F32, kind="Internal").ap()

    with ExitStack() as ctx:
        def sb(name, shape, dt=F32):
            return ctx.enter_context(nc.sbuf_tensor(name, shape, dt))

        def sem(name):
            return ctx.enter_context(nc.semaphore(name))

        ps = ctx.enter_context(nc.psum_tensor("ps", [P, 8, 512], F32))

        x = sb("x", [P, NB, D])
        acc = sb("acc", [P, NB + 1, ROW])
        kq = sb("kq", [P, 2, NB * P])
        adv = sb("adv", [P, NB, ADV])
        wbig = sb("wbig", [P, KC, HW])
        wqk = sb("wqk", [P, KC, 2 * QK])
        wout = sb("wout", [P, D])
        w1 = sb("w1", [P, KC, FF])
        w2 = sb("w2", [P, FC, D])
        b1 = sb("b1", [P, FC])
        b1r = sb("b1r", [FC, P])
        b2b = sb("b2b", [P, D])
        wrb = sb("wrb", [P, D])
        brb = sb("brb", [P, 1])
        boutb = sb("boutb", [P, D])
        avec = sb("avec", [P, 2, HF])
        stats = sb("stats", [P, BODY, 6])
        mv = sb("mv", [P, NB, 2])
        rstd = sb("rstd", [P, NB])
        sd = sb("sd", [P, NB])
        eps = sb("eps", [P, 1])
        xn = sb("xn", [P, BODY, D])
        xnT = sb("xnT", [P, BODY, KC, P])
        hst = sb("hst", [P, BODY, ROW])
        iota = sb("iota", [P, P])
        ident = sb("ident", [P, P])
        part = sb("part", [P, 1])
        tri = sb("tri", [P, P])
        nodeid = sb("nodeid", [P, NB])
        blkbase = sb("blkbase", [P, NB])
        ones = sb("ones", [1, P])
        zrow = sb("zrow", [1, 2 * P], BF16)
        zrow32 = sb("zrow32", [1, ROW])
        ad3 = sb("ad3", [P, NB, 3, HEADS], BF16)
        adr = sb("adr", [P, NB, 2, HEADS])
        dl = sb("dl", [NG, GE], I32)
        du = sb("du", [NG, GE], U16)
        mm = sb("mm", [NG, 2], I32)
        meta = sb("meta", [1, NG * 2], I32)
        srcc = sb("srcc", [P, NG + RING, TILES], I32)
        wc = sb("wc", [P, NG, TILES])
        dci = sb("dci", [P, NG, TILES], I32)
        dcf = sb("dcf", [P, NG, TILES])
        idxr = sb("idxr", [P, RING, TILES], I32)
        G = sb("G", [P, RING, TILES, ROW])
        free = G[:, :, :, :].rearrange("p q k c -> p (q k c)")
        aprod = free[:, 0:2 * KC * HF].rearrange("p (s c n) -> p s c n", s=2, c=KC)
        gsc = free[:, 0:BODY * D].rearrange("p (j n) -> p j n", j=BODY)
        yb = free[:, BODY * D:(BODY + 2) * D].rearrange("p (j n) -> p j n", j=2)
        ob = free[:, (BODY + 2) * D:(BODY + 6) * D].rearrange("p (j n) -> p j n", j=4)
        msg = sb("msg", [P, 2, TILES, ROW])
        oh = sb("oh", [P, 2, TILES, P])
        ohT = sb("ohT", [P, GE], BF16)
        dstb = sb("dstb", [P, RING, GE], U16)
        et = sb("et", [P, 2, 17])
        rm = sb("rm", [P, 2])
        rg = sb("rg", [1, 2])
        Rsb = sb("Rsb", [P, 2])
        negR = sb("negR", [P, 2])
        Rlast = sb("Rlast", [P, NB])
        fsc = sb("fsc", [P, 2])
        Fin = sb("Fin", [P, NB])
        kmax = sb("kmax", [P, 2])
        ksum = sb("ksum", [P, 2])
        ekt = sb("ekt", [P, BODY, P])
        ctxT = sb("ctxT", [P, P])
        C2 = sb("C2", [P, D])
        rden = sb("rden", [P, 2, NB, HEADS])
        wtok = sb("wtok", [P, NB])
        wprod = sb("wprod", [P, D])
        hT = sb("hT", [P, 2, FC, P])
        cnt = sb("cnt", [P, NB, 3])
        mw = sb("mw", [P, NB])
        rank = sb("rank", [P, NB])
        wrow = kq[:, 0, :]
        junk = kq[:, 1, :]
        wtT = sb("wtT", [NB, P])

        S = {}
        for name in ("const gp_go dve_go act_go sd ld_bo ld_w ld_bc ld_avec avs wbig st mv rstd xn tp xT h hst adv kqm kq xb "
                     "ld_dl ld_dc dlp dlst meta ld_e prep km ke ks ekT ek ctx ctxs c2 c2s mixm mix "
                     "idx s_ohT ad zc e ec T rg B R ex msg oh agg acc f facc fin "
                     "den gs x1 wt wtt wst wrow cnt rk x2 xn2 t2 x2T h1 g1 y yb fo acp accz "
                     ).split():
            S[name] = sem("s_" + name if not name.startswith("s_") else name)
        s_x = [sem(f"ld_x{i}") for i in range(NB // BODY)]
        s_tab = [sem(f"s_tab{i}") for i in range(BODY)]
        s_dstb = [sem(f"s_dstb{i}") for i in range(RING)]
        s_g = [sem(f"gathered{i}") for i in range(RING)]
        s_out = [sem(f"s_out{i}") for i in range(4)]

        block = ctx.enter_context(nc.Block())

        def groups(eng, step):
            for g in range(RING):
                step(g, g)
            with eng.Fori(1, LOOPS) as i:
                for q in range(RING):
                    step(i * RING + q, q)
            for g in range(LOOPS * RING, NG):
                step(g, g % RING)

        @block.sync
        def _(sp):
            with nc.allow_non_contiguous_dma(reason="weights, edge columns"):
                for i in range(NB // BODY):
                    lo = i * BODY
                    if i < NB // BODY - 1:
                        sp.dma_start(x[:, lo:lo + BODY, :], x_in[lo * P:(lo + BODY) * P, :].rearrange("(b p) c -> p b c", p=P)).then_inc(s_x[i], 16)
                    else:
                        sp.dma_start(x[:, lo:NB - 1, :], x_in[lo * P:(NB - 1) * P, :].rearrange("(b p) c -> p b c", p=P)).then_inc(s_x[i], 16)
                        sp.wait_ge(S["const"], 1)
                        sp.dma_start(x[0:REST, NB - 1, :], x_in[(NB - 1) * P:N, :]).then_inc(s_x[i], 16)
                    if i == 0:
                        for kc in range(KC):
                            sp.dma_start(wbig[:, kc, 0:HF].rearrange("k (h o) -> k h o", h=HEADS),
                                         gw_in[:, kc * P:(kc + 1) * P, :].rearrange("h k o -> k h o")).then_inc(S["ld_w"], 16)
                            sp.dma_start(wbig[:, kc, HW - QK:HW], wqkv_in[kc * P:(kc + 1) * P, 2 * QK:3 * QK]).then_inc(S["ld_w"], 16)
                            sp.dma_start(wqk[:, kc, :], wqkv_in[kc * P:(kc + 1) * P, 0:2 * QK]).then_inc(S["ld_w"], 16)
                        sp.dma_start(avec[:, 0, :], gas_in.rearrange("(a h) o b -> a (h o b)", a=1).to_broadcast([P, HF])).then_inc(S["ld_avec"], 16)
                        sp.dma_start(avec[:, 1, :], gad_in.rearrange("(a h) o b -> a (h o b)", a=1).to_broadcast([P, HF])).then_inc(S["ld_avec"], 16)
                        sp.dma_start(boutb[:, :], bout_in.rearrange("(a d) -> a d", a=1).to_broadcast([P, D])).then_inc(S["ld_bo"], 16)
                full = (NG - 1) * GE
                sp.dma_start(dl[0:NG - 1, :], dst_in[0:full].rearrange("(g j) -> g j", j=GE)).then_inc(S["ld_dl"], 16)
                sp.dma_start(dl[NG - 1:NG, 0:EREST], dst_in[full:E].rearrange("(g j) -> g j", g=1)).then_inc(S["ld_dl"], 16)
                sp.dma_start(dl[NG - 1:NG, EREST:GE], dst_in[E - PAD:E].rearrange("(g j) -> g j", g=1)).then_inc(S["ld_dl"], 16)
                sp.dma_start(srcc[:, 0:NG - 1, :], src_in[0:full].rearrange("(g p k) -> p g k", p=P, k=TILES)).then_inc(S["ld_e"], 16)
                sp.dma_start(srcc[0:PREST, NG - 1, :], src_in[full:E].rearrange("(p k) -> p k", k=TILES)).then_inc(S["ld_e"], 16)
                sp.dma_start(srcc[PREST:P, NG - 1, :], src_in[E - PAD:E].rearrange("(p k) -> p k", k=TILES)).then_inc(S["ld_e"], 16)
                sp.dma_start(wc[:, 0:NG - 1, :], ew_in[0:full].rearrange("(g p k) -> p g k", p=P, k=TILES)).then_inc(S["ld_e"], 16)
                sp.dma_start(wc[0:PREST, NG - 1, :], ew_in[full:E].rearrange("(p k) -> p k", k=TILES)).then_inc(S["ld_e"], 16)
                sp.dma_start(wc[PREST:P, NG - 1, :], ew_in[E - PAD:E].rearrange("(p k) -> p k", k=TILES)).then_inc(S["ld_e"], 16)
                sp.dma_start(dci[:, 0:NG - 1, :], dst_in[0:full].rearrange("(g p k) -> p g k", p=P, k=TILES)).then_inc(S["ld_dc"], 16)
                sp.dma_start(dci[0:PREST, NG - 1, :], dst_in[full:E].rearrange("(p k) -> p k", k=TILES)).then_inc(S["ld_dc"], 16)
                for t in range(NB):
                    sp.wait_ge(S["hst"], t + 1)
                    sp.dma_start(htab[t * P:(t + 1) * P, :], hst[:, t % BODY, :]).then_inc(s_tab[t % BODY], 16)
                sp.wait_ge(S["dlp"], 5)
                sp.dma_start(dstu_d[:, :], du[:, :]).then_inc(S["dlst"], 16)
                sp.dma_start(meta_d[:, :], mm[:, :]).then_inc(S["dlst"], 16)
                sp.wait_ge(S["dlst"], 32)
                sp.dma_start(meta[:, :], meta_d.rearrange("(a g) c -> a (g c)", a=1)).then_inc(S["meta"], 16)
                sp.dma_start(wout[:, :], wout_in).then_inc(S["ld_bc"], 16)
                sp.dma_start(w1[:, :, :], w1_in.rearrange("(c k) f -> k c f", k=P)).then_inc(S["ld_bc"], 16)
                sp.dma_start(w2[:, :, :], w2_in.rearrange("(c k) f -> k c f", k=P)).then_inc(S["ld_bc"], 16)
                sp.dma_start(b1r[:, :], b1_in.rearrange("(c k) -> c k", k=P)).then_inc(S["ld_bc"], 16)
                sp.dma_start(b2b[:, :], b2_in.rearrange("(a d) -> a d", a=1).to_broadcast([P, D])).then_inc(S["ld_bc"], 16)
                sp.dma_start(wrb[:, :], wr_in.rearrange("d (a b) -> a (d b)", a=1).to_broadcast([P, D])).then_inc(S["ld_bc"], 16)
                sp.dma_start(brb[:, :], br_in.rearrange("(a b) -> a b", a=1).to_broadcast([P, 1])).then_inc(S["ld_bc"], 16)

                def step(g, q):
                    if not (isinstance(g, int) and g < RING):
                        sp.wait_ge(S["e"], g - RING + 1)
                    sp.dma_start(dstb[:, q, :], dstu_d[bass.ds(g, 1), :].to_broadcast([P, GE])).then_inc(s_dstb[q], 16)
                groups(sp, step)

                sp.wait_ge(S["wtt"], 1)
                sp.dma_start(w_d[:, :], wtT[:, :]).then_inc(S["wst"], 16)
                sp.wait_ge(S["wst"], 16)
                sp.dma_start(wrow, w_d.rearrange("(a b) p -> a (b p)", a=1).to_broadcast([P, NB * P])).then_inc(S["wrow"], 16)
                for t in range(NB):
                    rows = P if t < NB - 1 else REST
                    sp.wait_ge(S["fo"], t + 1)
                    sp.dma_start(out[t * P:t * P + rows, :], ob[0:rows, t % 4, :]).then_inc(s_out[t % 4], 16)
                for k in range(4):
                    sp.wait_ge(s_out[k], 16 * len(range(k, NB, 4)))

        @block.gpsimd
        def _(gp):
            gp.memset(x[:, NB - 1, :], 0.0).then_inc(S["const"], 1)
            gp.iota(iota[:, :], [[1, P]], base=0, channel_multiplier=0, allow_small_or_imprecise_dtypes=True).then_inc(S["const"], 1)
            gp.iota(part[:, :], [[0, 1]], base=0, channel_multiplier=1, allow_small_or_imprecise_dtypes=True).then_inc(S["const"], 1)
            gp.iota(nodeid[:, :], [[P, NB]], base=0, channel_multiplier=1, allow_small_or_imprecise_dtypes=True).then_inc(S["const"], 1)
            gp.iota(blkbase[:, :], [[P, NB]], base=0, channel_multiplier=0, allow_small_or_imprecise_dtypes=True).then_inc(S["const"], 1)
            gp.memset(eps[:, :], LN_EPS).then_inc(S["const"], 1)
            gp.memset(ones[:, :], 1.0).then_inc(S["const"], 1)
            gp.memset(zrow[:, :], 0.0).then_inc(S["const"], 1)
            gp.memset(zrow32[:, :], 0.0).then_inc(S["const"], 1)
            gp.memset(et[:, :, :], LOWEST).then_inc(S["const"], 1)
            gp.memset(Rlast[:, :], LOWEST).then_inc(S["const"], 1)
            gp.memset(fsc[:, :], 0.0).then_inc(S["const"], 1)
            gp.memset(ctxT[:, :], 0.0).then_inc(S["const"], 1)
            gp.memset(srcc[:, NG:NG + RING, :], 0).then_inc(S["const"], 1)
            gp.memset(acc[:, :, :], 0.0).then_inc(S["accz"], 1)
            gp.wait_ge(S["ld_bo"], 16)
            for t in range(NB):
                gp.wait_ge(S["xn"], t + 1)
                gp.tensor_tensor(x[:, t, :], x[:, t, :], boutb[:, :], ALU.add).then_inc(S["xb"], 1)
            for j in range(BODY):
                gp.wait_ge(s_tab[j], 16 * (NB // BODY))

            def step(g, q):
                gp.wait_ge(S["idx"], g + 1)
                gp.sem_inc(S["gp_go"], 1)
                for k in range(TILES):
                    gp.indirect_dma_start(G[:, q, k, :], None, htab, bass.IndirectOffsetOnAxis(ap=idxr[:, q, k:k + 1], axis=0)).then_inc(s_g[q], 16)
            groups(gp, step)

        @block.tensor
        def _(pe):
            pe.wait_ge(S["const"], 15)
            pe.wait_ge(S["ld_w"], 32 * 3)
            pe.wait_ge(S["wbig"], 1)

            def project(t):
                b = t % 2
                pe.wait_ge(S["xT"], t + 1)
                if t >= 2:
                    pe.wait_ge(S["adv"], t - 1)
                for kc in range(KC):
                    m = pe.matmul(ps[:, 2 + b, 0:HW], xnT[:, t % BODY, kc, :], wbig[:, kc, :], start=(kc == 0), stop=(kc == KC - 1))
                m.then_inc(S["h"], 1)
                if t >= 2:
                    pe.wait_ge(S["kq"], t - 1)
                for c in range(2):
                    for kc in range(KC):
                        m = pe.matmul(ps[:, 4 + b, c * P:(c + 1) * P], wqk[:, kc, (1 - c) * P:(2 - c) * P], xnT[:, t % BODY, kc, :],
                                      start=(kc == 0), stop=(kc == KC - 1))
                m.then_inc(S["kqm"], 1)

            for t in range(NB):
                pe.wait_ge(S["xn"], t + 1)
                if t >= 2:
                    pe.wait_ge(S["xT"], t - 1)
                for kc in range(KC):
                    m = pe.transpose(ps[:, t % 2, kc * P:(kc + 1) * P], xn[:, t % BODY, kc * P:(kc + 1) * P], ident[:, :])
                m.then_inc(S["tp"], 1)
                if t:
                    project(t - 1)
            project(NB - 1)

            for t in range(NB + 1):
                if t < NB:
                    if t == 0:
                        pe.wait_ge(S["ke"], 2)
                    if t >= 2:
                        pe.wait_ge(S["ek"], t - 1)
                    pe.transpose(ps[:, t % 2, 0:P], kq[:, 0, t * P:(t + 1) * P], ident[:, :]).then_inc(S["ekT"], 1)
                if t:
                    u = t - 1
                    pe.wait_ge(S["ek"], u + 1)
                    if u == 0:
                        pe.wait_ge(S["adv"], NB)
                    pe.matmul(ps[:, 6, 0:P], adv[:, u, HEADS:ADV], ekt[:, u % BODY, :], start=(u == 0), stop=(u == NB - 1)).then_inc(S["ctx"], 1)
            pe.wait_ge(S["ctxs"], MIX_HEADS)
            pe.wait_ge(S["ld_bc"], 16 * 7)
            pe.matmul(ps[:, 7, 0:D], ctxT[:, :], wout[:, :], start=True, stop=True).then_inc(S["c2"], 1)
            pe.wait_ge(S["c2s"], 1)
            for t in range(NB):
                if t >= 2:
                    pe.wait_ge(S["mix"], t - 1)
                pe.matmul(ps[:, 2 + t % 2, 0:D], kq[:, 1, t * P:(t + 1) * P], C2[:, :], start=True, stop=True).then_inc(S["mixm"], 1)
            pe.wait_ge(S["kq"], NB)
            pe.transpose(ps[:, 5, 0:FC], b1r[:, :], ident[0:FC, 0:FC]).then_inc(S["c2"], 1)

            pe.wait_ge(S["meta"], 16)
            pe.wait_ge(S["mix"], NB)
            pe.matmul(ps[:, 4, 0:ROW], zrow32[:, 0:P], zrow32[:, 0:ROW], start=True, stop=True).then_inc(S["agg"], 1)
            pe.matmul(ps[0:P, 2, 300:301], zrow32[:, 0:P], zrow32[:, 0:1], start=True, stop=True).then_inc(S["ad"], 1)
            va = pe.alloc_register()
            v = pe.alloc_register()
            w = pe.alloc_register()
            pe.reg_mov(va, 1)
            pe.reg_mov(v, 1)
            pe.wait_ge(S["prep"], 1)
            pe.wait_ge(S["c2s"], 2)

            def expand(g):
                p = g % 2 if isinstance(g, int) else None
                return p

            def ad_of(g, p):
                b0 = pe.value_load(meta[0:1, bass.ds(2 * g, 1)], min_val=0, max_val=NB - 1)
                b1_ = pe.value_load(meta[0:1, bass.ds(2 * g + 1, 1)], min_val=1, max_val=NB)
                if not (isinstance(g, int) and g < 2):
                    pe.wait_ge(S["e"], g - 1)
                pe.matmul(ps[:, p, 0:16], zrow[:, 0:P], zrow[:, 0:16], start=True, stop=False, skip_group_check=True)
                with pe.Fori(b0, b1_) as b:
                    pe.wait_ge(S["s_ohT"], va)
                    for k in range(TILES):
                        for j in range(3):
                            m = pe.matmul(ps[:, p, 4 * k:4 * k + 4], ohT[:, k:GE:TILES], ad3[:, bass.ds(b, 1), j, :].rearrange("p a h -> p (a h)"),
                                          start=False, stop=False, skip_group_check=True)
                    m.then_inc(S["ad"], 1)
                    pe.reg_add(va, va, 1)

            def max_of(g, p):
                pe.wait_ge(S["e"], g + 1)
                if not (isinstance(g, int) and g < 1):
                    pe.wait_ge(S["rg"], g)
                pe.transpose(ps[0:1, 2, 0:P], rm[:, p:p + 1], ident[:, :]).then_inc(S["T"], 1)
                pe.wait_ge(S["rg"], g + 1)
                if not (isinstance(g, int) and g < 1):
                    pe.wait_ge(S["ex"], g)
                pe.matmul(ps[:, 5, 0:1], ones[:, :], rg[:, p:p + 1], start=True, stop=True).then_inc(S["B"], 1)

            def sums(g, p):
                b0 = pe.value_load(meta[0:1, bass.ds(2 * g, 1)], min_val=0, max_val=NB - 1)
                b1_ = pe.value_load(meta[0:1, bass.ds(2 * g + 1, 1)], min_val=1, max_val=NB)
                pe.wait_ge(S["msg"], g + 1)
                pe.reg_mov(w, v)
                with pe.Fori(b0, b1_) as b:
                    pe.wait_ge(S["acc"], w)
                    pe.wait_ge(S["oh"], v)
                    for k in range(TILES):
                        m = pe.matmul(ps[:, 3 + p, 0:ROW], oh[:, p, k, :], msg[:, p, k, :], start=(k == 0), stop=(k == TILES - 1))
                    m.then_inc(S["agg"], 1)
                    pe.reg_add(v, v, 1)
                    pe.reg_add(w, v, 1)

            ad_of(0, 0)
            ad_of(1, 1)
            max_of(0, 0)

            def step(g, q):
                last = isinstance(g, int)
                if not (last and g + 2 >= NG):
                    ad_of(g + 2, q % 2)
                if not (last and g + 1 >= NG):
                    max_of(g + 1, (q + 1) % 2)
                sums(g, q % 2)
            groups(pe, step)

            pe.wait_ge(S["wt"], NB)
            pe.transpose(ps[0:NB, 7, 0:P], wtok[:, :], ident[:, :]).then_inc(S["t2"], 1)

            def up(t):
                pe.wait_ge(S["x2T"], t + 1)
                if t >= 1:
                    pe.wait_ge(S["g1"], t)
                for c in range(FC):
                    for kc in range(KC):
                        m = pe.matmul(ps[:, 2 + c // 4, (c % 4) * P:(c % 4 + 1) * P], w1[:, kc, c * P:(c + 1) * P], xnT[:, t % BODY, kc, :],
                                      start=(kc == 0), stop=(kc == KC - 1))
                m.then_inc(S["h1"], 1)

            def down(t):
                pe.wait_ge(S["g1"], t + 1)
                if t >= 2:
                    pe.wait_ge(S["yb"], t - 1)
                for c in range(FC):
                    m = pe.matmul(ps[:, 4 + t % 2, 0:D], hT[:, t % 2, c, :], w2[:, c, :], start=(c == 0), stop=(c == FC - 1))
                m.then_inc(S["y"], 1)

            for t in range(NB + 1):
                if t < NB:
                    pe.wait_ge(S["xn2"], t + 1)
                    if t >= 2:
                        pe.wait_ge(S["x2T"], t - 1)
                    for kc in range(KC):
                        m = pe.transpose(ps[:, t % 2, kc * P:(kc + 1) * P], xn[:, t % BODY, kc * P:(kc + 1) * P], ident[:, :])
                    m.then_inc(S["t2"], 1)
                    up(t)
                if t:
                    down(t - 1)

        @block.scalar
        def _(act):
            act.wait_ge(S["const"], 15)

            def deviation(base, n, mvs):
                act.wait_ge(S["mv"], mvs)
                act.activation(sd[:, base:base + n], mv[:, base:base + n, 1:2].rearrange("p a b -> p (a b)"), ACT.Sqrt, bias=eps[:, 0:1]).then_inc(S["sd"], 1)

            def evacuate_kq(t):
                act.wait_ge(S["kqm"], t + 1)
                act.activation(kq[:, :, t * P:(t + 1) * P], ps[:, 4 + t % 2, 0:2 * P].rearrange("p (c n) -> p c n", c=2), ACT.Copy).then_inc(S["kq"], 1)

            deviation(0, BODY, BODY)
            for t in range(NB):
                if t % BODY == 2 and t + BODY < NB:
                    deviation(t - 2 + BODY, BODY, t - 2 + 2 * BODY)
                act.wait_ge(S["tp"], t + 1)
                if t >= BODY:
                    act.wait_ge(S["kqm"], t - BODY + 1)
                act.activation(xnT[:, t % BODY, :, :], ps[:, t % 2, 0:D].rearrange("p (c n) -> p c n", c=KC), ACT.Copy).then_inc(S["xT"], 1)
                if t:
                    evacuate_kq(t - 1)
            evacuate_kq(NB - 1)

            act.wait_ge(S["km"], 2)
            act.activation(kq[:, 0, 0:N], kq[:, 0, 0:N], ACT.Exp, bias=kmax[:, 1:2], accum_out=ksum[:, 0:1]).then_inc(S["ke"], 1)
            for t in range(NB):
                act.wait_ge(S["ekT"], t + 1)
                if t >= BODY:
                    act.wait_ge(S["ctx"], t - BODY + 1)
                act.activation(ekt[:, t % BODY, :], ps[:, t % 2, 0:P], ACT.Copy).then_inc(S["ek"], 1)
            act.wait_ge(S["c2"], 2)
            act.activation(b1[:, :], ps[:, 5, 0:FC], ACT.Copy).then_inc(S["c2s"], 1)

            act.wait_ge(S["meta"], 16)
            v = act.alloc_register()
            u = act.alloc_register()
            w = act.alloc_register()
            act.reg_mov(v, 1)
            act.reg_mov(u, 1)

            def step(g, q):
                p = q % 2
                b0 = act.value_load(meta[0:1, bass.ds(2 * g, 1)], min_val=0, max_val=NB - 1)
                b1_ = act.value_load(meta[0:1, bass.ds(2 * g + 1, 1)], min_val=1, max_val=NB)
                act.wait_ge(S["B"], g + 1)
                act.activation(Rsb[:, p:p + 1], ps[:, 5, 0:1], ACT.Copy).then_inc(S["facc"], 1)
                act.activation(et[:, 1 - p, 16:17], ps[:, 5, 0:1], ACT.Copy).then_inc(S["R"], 1)
                act.activation(negR[:, p:p + 1], ps[:, 5, 0:1], ACT.Copy, scale=-1.0).then_inc(S["facc"], 1)
                act.wait_ge(S["agg"], u)
                act.wait_ge(S["facc"], 2 * g + 2)
                act.activation(msg[:, p, :, HF:ROW], et[:, p, 0:16].rearrange("p (k h) -> p k h", k=TILES), ACT.Exp, bias=negR[:, p:p + 1]).then_inc(S["ex"], 1)
                act.reg_mov(u, v)
                act.reg_mov(w, v)
                with act.Fori(b0, b1_) as b:
                    act.wait_ge(S["acc"], w)
                    act.wait_ge(S["fin"], v)
                    act.reg_add(w, v, 1)
                    act.sem_inc(S["act_go"], 1)
                    act.activation(fsc[:, p:p + 1], Rlast[:, bass.ds(b, 1)], ACT.Exp, bias=negR[:, p:p + 1]).then_inc(S["f"], 1)
                    act.wait_ge(S["f"], w)
                    act.sem_inc(S["act_go"], 1)
                    act.activation(Rlast[:, bass.ds(b, 1)], Rsb[:, p:p + 1], ACT.Copy).then_inc(S["fin"], 1)
                    act.reg_add(v, v, 1)
                    act.reg_add(w, v, 1)
            act.sem_inc(S["acc"], 1)
            act.sem_inc(S["f"], 1)
            act.sem_inc(S["fin"], 1)
            groups(act, step)
            act.wait_ge(S["fin"], v)
            act.activation(Fin[:, :], Rlast[:, :], ACT.Exp, bias=negR[:, (NG - 1) % 2:(NG - 1) % 2 + 1]).then_inc(S["den"], 1)

            deviation(0, NB, 2 * NB)
            act.wait_ge(S["t2"], 1)
            act.activation(wtT[:, :], ps[0:NB, 7, 0:P], ACT.Copy).then_inc(S["wtt"], 1)
            for t in range(NB):
                act.wait_ge(S["t2"], t + 2)
                if t >= BODY:
                    act.wait_ge(S["h1"], t - BODY + 1)
                act.activation(xnT[:, t % BODY, :, :], ps[:, t % 2, 0:D].rearrange("p (c n) -> p c n", c=KC), ACT.Copy).then_inc(S["x2T"], 1)
                act.wait_ge(S["h1"], t + 1)
                if t >= 2:
                    act.wait_ge(S["y"], t - 1)
                for c in range(FC):
                    m = act.activation(hT[:, t % 2, c, :], ps[:, 2 + c // 4, (c % 4) * P:(c % 4 + 1) * P], ACT.Gelu_apprx_tanh, bias=b1[:, c:c + 1])
                m.then_inc(S["g1"], 1)

        @block.vector
        def _(dve):
            dve.wait_ge(S["const"], 14)
            dve.tensor_scalar(ident[:, :], iota[:, :], part[:, 0:1], None, ALU.is_equal).then_inc(S["const"], 1)
            dve.tensor_scalar(tri[:, :], iota[:, :], part[:, 0:1], None, ALU.is_lt).then_inc(S["fo"], 0) if False else dve.tensor_scalar(tri[:, :], iota[:, :], part[:, 0:1], None, ALU.is_lt)
            dve.wait_ge(S["ld_avec"], 32)
            dve.wait_ge(S["ld_w"], 32 * 3)
            for s in range(2):
                dve.tensor_tensor(aprod[:, s, :, :], wbig[:, :, 0:HF], avec[:, s:s + 1, :].to_broadcast([P, KC, HF]), ALU.mult).then_inc(S["avs"], 1)
            dve.wait_ge(S["avs"], 2)
            for s in range(2):
                m = dve.tensor_reduce(wbig[:, :, HF + s * HEADS:HF + (s + 1) * HEADS], aprod[:, s, :, :].rearrange("p c (h o) -> p c h o", h=HEADS), AX.X, ALU.add)
            m.then_inc(S["wbig"], 1)

            def statistics(base, n, st0):
                for j in range(n):
                    dve.bn_stats(stats[:, j, :], x[:, base + j, :]).then_inc(S["st"], 1)
                dve.wait_ge(S["st"], st0 + n)
                for j in range(n):
                    dve.bn_aggr(mv[:, base + j, :], stats[:, j, :]).then_inc(S["mv"], 1)

            def invert(base, n, k):
                dve.wait_ge(S["sd"], k)
                dve.reciprocal(rstd[:, base:base + n], sd[:, base:base + n]).then_inc(S["rstd"], 1)
                dve.wait_ge(S["rstd"], k)

            def normed(t):
                return dve.tensor_scalar(xn[:, t % BODY, :], x[:, t, :], mv[:, t, 0:1], rstd[:, t:t + 1], ALU.subtract, ALU.mult)

            def evacuate_h(t):
                dve.wait_ge(S["h"], t + 1)
                if t >= BODY:
                    dve.wait_ge(s_tab[t % BODY], 16 * (t // BODY))
                dve.tensor_copy(hst[:, t % BODY, :], ps[:, 2 + t % 2, 0:ROW]).then_inc(S["hst"], 1)
                dve.tensor_copy(adv[:, t, :], ps[:, 2 + t % 2, ROW:HW]).then_inc(S["adv"], 1)

            for i in range(NB // BODY):
                dve.wait_ge(s_x[i], 16 if i < NB // BODY - 1 else 32)
                statistics(i * BODY, BODY, i * BODY)
                invert(i * BODY, BODY, i + 1)
                for j in range(BODY):
                    t = i * BODY + j
                    if t >= BODY:
                        dve.wait_ge(S["tp"], t - BODY + 1)
                    normed(t).then_inc(S["xn"], 1)
                    if t >= 3:
                        evacuate_h(t - 3)
            for t in range(NB - 3, NB):
                evacuate_h(t)

            dve.wait_ge(S["ld_dl"], 48)
            dve.tensor_copy(du[:, :], dl[:, :]).then_inc(S["dlp"], 1)
            dve.tensor_reduce(mm[:, 0:1], dl[:, :], AX.X, ALU.min).then_inc(S["dlp"], 1)
            dve.tensor_reduce(mm[:, 1:2], dl[:, :], AX.X, ALU.max).then_inc(S["dlp"], 1)
            dve.wait_ge(S["dlp"], 3)
            dve.tensor_scalar(mm[:, :], mm[:, :], 7, None, ALU.arith_shift_right).then_inc(S["dlp"], 1)
            dve.wait_ge(S["dlp"], 4)
            dve.tensor_scalar(mm[:, 1:2], mm[:, 1:2], 1, None, ALU.add).then_inc(S["dlp"], 1)
            dve.memset(dcf[:, NG - 1, :], -1.0).then_inc(S["zc"], 1)
            dve.wait_ge(S["ld_dc"], 32)
            dve.tensor_copy(dcf[:, 0:NG - 1, :], dci[:, 0:NG - 1, :]).then_inc(S["zc"], 1)
            dve.wait_ge(S["zc"], 1)
            dve.tensor_copy(dcf[0:PREST, NG - 1, :], dci[0:PREST, NG - 1, :]).then_inc(S["zc"], 1)
            dve.wait_ge(S["ld_e"], 96)
            for q in range(RING):
                dve.tensor_copy(idxr[:, q, :], srcc[:, q, :]).then_inc(S["idx"], 1)
            dve.wait_ge(S["adv"], NB)
            dve.tensor_copy(ad3[:, :, 0, :], adv[:, :, 0:HEADS]).then_inc(S["acp"], 1)
            dve.wait_ge(S["acp"], 1)
            dve.tensor_tensor(adr[:, :, 0, :], adv[:, :, 0:HEADS], ad3[:, :, 0, :], ALU.subtract).then_inc(S["acp"], 1)
            dve.wait_ge(S["acp"], 2)
            dve.tensor_copy(ad3[:, :, 1, :], adr[:, :, 0, :]).then_inc(S["acp"], 1)
            dve.wait_ge(S["acp"], 3)
            dve.tensor_tensor(adr[:, :, 1, :], adr[:, :, 0, :], ad3[:, :, 1, :], ALU.subtract).then_inc(S["acp"], 1)
            dve.wait_ge(S["acp"], 4)
            dve.tensor_copy(ad3[:, :, 2, :], adr[:, :, 1, :]).then_inc(S["prep"], 1)

            dve.wait_ge(S["kq"], NB)
            dve.tensor_reduce(kmax[:, 0:1], kq[:, 0, 0:N], AX.X, ALU.max).then_inc(S["km"], 1)
            dve.wait_ge(S["km"], 1)
            dve.tensor_scalar(kmax[:, 1:2], kmax[:, 0:1], -1.0, None, ALU.mult).then_inc(S["km"], 1)
            dve.memset(kq[:, 0, N:NB * P], 0.0).then_inc(S["ke"], 1)
            dve.wait_ge(S["ke"], 2)
            dve.reciprocal(ksum[:, 1:2], ksum[:, 0:1]).then_inc(S["ks"], 1)
            dve.wait_ge(S["ctx"], NB)
            for h in range(MIX_HEADS):
                s = slice(h * DIM_HEAD, (h + 1) * DIM_HEAD)
                dve.tensor_copy(ctxT[s, s], ps[s, 6, s]).then_inc(S["ctxs"], 1)
            dve.wait_ge(S["c2"], 1)
            dve.wait_ge(S["ks"], 1)
            dve.tensor_scalar(C2[:, :], ps[:, 7, 0:D], ksum[:, 1:2], float(DIM_HEAD) ** -0.5, ALU.mult, ALU.mult).then_inc(S["c2s"], 1)
            dve.wait_ge(S["xb"], NB)
            for t in range(NB):
                dve.wait_ge(S["mixm"], t + 1)
                dve.tensor_tensor(x[:, t, :], ps[:, 2 + t % 2, 0:D], x[:, t, :], ALU.add).then_inc(S["mix"], 1)

            dve.wait_ge(S["meta"], 16)
            dve.wait_ge(S["accz"], 1)
            va = dve.alloc_register()
            vw = dve.alloc_register()
            v = dve.alloc_register()
            w = dve.alloc_register()
            vold = dve.alloc_register()
            pb = dve.alloc_register()
            pp = dve.alloc_register()
            for r, val in ((va, 1), (v, 1), (vold, 1), (pb, NB), (pp, 1)):
                dve.reg_mov(r, val)

            def columns(g, q):
                b0 = dve.value_load(meta[0:1, bass.ds(2 * g, 1)], min_val=0, max_val=NB - 1)
                b1_ = dve.value_load(meta[0:1, bass.ds(2 * g + 1, 1)], min_val=1, max_val=NB)
                dve.reg_mov(vw, va)
                dve.wait_ge(s_dstb[q], 16 * ((g - q) // RING + 1) if isinstance(g, int) else (g - q) * (16 // RING) + 16)
                dve.sem_inc(S["dve_go"], 1)
                with dve.Fori(b0, b1_) as b:
                    dve.wait_ge(S["ad"], va)
                    dve.tensor_scalar(ohT[:, :], dstb[:, q, :], nodeid[:, bass.ds(b, 1)], None, ALU.is_equal).then_inc(S["s_ohT"], 1)
                    dve.reg_add(va, va, 1)

            def logits(g, q, cols):
                p = q % 2
                dve.wait_ge(s_g[q], 64 * ((g - q) // RING + 1) if isinstance(g, int) else (g - q) * (64 // RING) + 64)
                dve.wait_ge(S["ad"], vw)
                e16 = et[:, p, 0:16].rearrange("p (k h) -> p k h", k=TILES)
                dve.tensor_tensor(e16, ps[:, p, 0:16].rearrange("p (k h) -> p k h", k=TILES), G[:, q, :, HF:ROW], ALU.add).then_inc(S["ec"], 1)
                dve.wait_ge(S["ec"], 3 * g + 1)
                dve.scalar_tensor_tensor(out=et[:, p, 0:16], in0=et[:, p, 0:16], scalar=NEG_SLOPE, in1=et[:, p, 0:16], op0=ALU.mult, op1=ALU.max).then_inc(S["ec"], 1)
                dve.wait_ge(S["ec"], 3 * g + 2)
                wg = wc[:, bass.ds(g, 1), :].rearrange("p a k -> p (a k)").unsqueeze(2).to_broadcast([P, TILES, HEADS])
                dve.tensor_tensor(e16, e16, wg, ALU.mult).then_inc(S["ec"], 1)
                dve.wait_ge(S["ec"], 3 * g + 3)
                if not (isinstance(g, int) and g < 1):
                    dve.wait_ge(S["R"], g)
                dve.tensor_reduce(rm[:, p:p + 1], et[:, p, 0:17], AX.X, ALU.max).then_inc(S["e"], 1)

            def group_max(g, q):
                p = q % 2
                dve.wait_ge(S["T"], g + 1)
                dve.tensor_reduce(rg[:, p:p + 1], ps[0:1, 2, 0:P], AX.X, ALU.max).then_inc(S["rg"], 1)

            def messages(g, q):
                p = q % 2
                dve.wait_ge(S["ex"], g + 1)
                ex = msg[:, p, :, HF:ROW].unsqueeze(3).to_broadcast([P, TILES, HEADS, OUT_F])
                dve.tensor_tensor(msg[:, p, :, 0:HF].rearrange("p k (h o) -> p k h o", h=HEADS),
                                  G[:, q, :, 0:HF].rearrange("p k (h o) -> p k h o", h=HEADS), ex, ALU.mult).then_inc(S["msg"], 1)
                if not (isinstance(g, int) and g + RING >= NG):
                    dve.wait_ge(S["msg"], g + 1)
                    dve.tensor_copy(idxr[:, q, :], srcc[:, bass.ds(g + RING, 1), :].rearrange("p a k -> p (a k)")).then_inc(S["idx"], 1)

            def add_previous():
                b = dve.snap(pb)
                s = dve.snap(pp)
                dve.wait_ge(S["agg"], v)
                dve.wait_ge(S["f"], v)
                dve.wait_ge(S["acc"], v)
                a = acc[:, bass.ds(b, 1), :].rearrange("p a c -> p (a c)")
                dve.scalar_tensor_tensor(out=a, in0=a, scalar=fsc[:, bass.ds(s, 1)], in1=ps[:, bass.ds(s + 3, 1), 0:ROW].rearrange("p a c -> p (a c)"),
                                         op0=ALU.mult, op1=ALU.add).then_inc(S["acc"], 1)

            def visit(g, q):
                p = q % 2
                b0 = dve.value_load(meta[0:1, bass.ds(2 * g, 1)], min_val=0, max_val=NB - 1)
                b1_ = dve.value_load(meta[0:1, bass.ds(2 * g + 1, 1)], min_val=1, max_val=NB)
                dve.reg_mov(w, vold)
                with dve.Fori(b0, b1_) as b:
                    dve.wait_ge(S["agg"], w)
                    for k in range(TILES):
                        col = dcf[:, bass.ds(g, 1), k:k + 1].rearrange("p a k -> p (a k)")
                        m = dve.tensor_scalar(oh[:, p, k, :], iota[:, :], blkbase[:, bass.ds(b, 1)], col, ALU.add, ALU.is_equal)
                    m.then_inc(S["oh"], 1)
                    add_previous()
                    dve.reg_mov(pb, b)
                    dve.reg_mov(pp, p)
                    dve.reg_mov(vold, v)
                    dve.reg_add(v, v, 1)
                    dve.reg_mov(w, v)

            columns(0, 0)
            columns(1, 1)
            dve.reg_mov(vw, va)
            logits(0, 0, None)
            group_max(0, 0)

            def step(g, q):
                last = isinstance(g, int)
                if not (last and g + 2 >= NG):
                    columns(g + 2, (q + 2) % RING)
                elif g + 2 == NG:
                    dve.reg_mov(vw, va)
                if not (last and g + 1 >= NG):
                    logits(g + 1, (q + 1) % RING, None)
                messages(g, q)
                if not (last and g + 1 >= NG):
                    group_max(g + 1, (q + 1) % RING)
                visit(g, q)
            groups(dve, step)
            add_previous()
            dve.reg_add(w, v, 1)
            dve.wait_ge(S["acc"], w)

            dve.wait_ge(S["den"], 1)
            fb = Fin[:, :].unsqueeze(2).to_broadcast([P, NB, HEADS])
            dve.tensor_tensor(rden[:, 0, :, :], acc[:, 0:NB, HF:ROW], fb, ALU.mult).then_inc(S["gs"], 1)
            dve.wait_ge(S["gs"], 1)
            dve.tensor_scalar(rden[:, 1, :, :], rden[:, 0, :, :], DEN_EPS, None, ALU.add).then_inc(S["gs"], 1)
            dve.wait_ge(S["gs"], 2)
            dve.reciprocal(rden[:, 0, :, :], rden[:, 1, :, :]).then_inc(S["gs"], 1)
            dve.wait_ge(S["gs"], 3)
            dve.tensor_tensor(rden[:, 1, :, :], rden[:, 0, :, :], fb, ALU.mult).then_inc(S["gs"], 1)
            dve.wait_ge(S["gs"], 4)
            for i in range(NB // BODY):
                for j in range(BODY):
                    t = i * BODY + j
                    r = rden[:, 1, t, :].unsqueeze(2).to_broadcast([P, HEADS, OUT_F])
                    dve.tensor_tensor(gsc[:, j, :].rearrange("p (h o) -> p h o", h=HEADS), acc[:, t, 0:HF].rearrange("p (h o) -> p h o", h=HEADS), r, ALU.mult).then_inc(S["x1"], 1)
                dve.wait_ge(S["x1"], 2 * BODY * i + BODY)
                for j in range(BODY):
                    t = i * BODY + j
                    dve.tensor_tensor(x[:, t, :], x[:, t, :], gsc[:, j, :], ALU.add).then_inc(S["x1"], 1)
                dve.wait_ge(S["x1"], 2 * BODY * (i + 1))
                statistics(i * BODY, BODY, NB + i * BODY)
            invert(0, NB, NB // BODY + 1)
            for i in range(NB // BODY):
                for j in range(BODY):
                    t = i * BODY + j
                    xa = acc[:, t, 0:D]
                    dve.tensor_scalar(xa, x[:, t, :], mv[:, t, 0:1], rstd[:, t:t + 1], ALU.subtract, ALU.mult).then_inc(S["x2"], 1)
                dve.wait_ge(S["x2"], 2 * i * BODY + BODY)
                for j in range(BODY):
                    t = i * BODY + j
                    xa = acc[:, t, 0:D]
                    if t:
                        dve.wait_ge(S["wt"], t)
                    dve.tensor_tensor_reduce(wprod[:, :], xa, wrb[:, :], 1.0, brb[:, 0:1], ALU.mult, ALU.add, wtok[:, t:t + 1]).then_inc(S["wt"], 1)
                    dve.tensor_tensor(x[:, t, :], x[:, t, :], xa, ALU.add).then_inc(S["x2"], 1)

            def to_xn(t):
                if t >= BODY:
                    dve.wait_ge(S["t2"], t - BODY + 2)
                dve.tensor_copy(xn[:, t % BODY, :], acc[:, t, 0:D]).then_inc(S["xn2"], 1)

            for t in range(BODY):
                to_xn(t)
            dve.wait_ge(S["wrow"], 16)
            n = 0
            for t in range(NB):
                wt = wtok[:, t:t + 1]
                lo, hi = t * P, min((t + 1) * P, N)
                if t:
                    dve.wait_ge(S["cnt"], 3 * t)
                    dve.tensor_scalar(junk[:, 0:lo], wrow[:, 0:lo], wt, 0.0, ALU.is_ge, ALU.add, accum_out=cnt[:, t, 0:1]).then_inc(S["cnt"], 1)
                else:
                    dve.memset(cnt[:, t, 0:1], 0.0).then_inc(S["cnt"], 1)
                dve.tensor_scalar(junk[:, lo:N], wrow[:, lo:N], wt, 0.0, ALU.is_gt, ALU.add, accum_out=cnt[:, t, 1:2]).then_inc(S["cnt"], 1)
                dve.scalar_tensor_tensor(out=wprod[:, 0:hi - lo], in0=wrow[:, lo:hi], scalar=wt, in1=tri[:, 0:hi - lo], op0=ALU.is_equal, op1=ALU.mult, accum_out=cnt[:, t, 2:3]).then_inc(S["cnt"], 1)
                dve.wait_ge(S["cnt"], 3 * t + 3)
                dve.tensor_reduce(rank[:, t:t + 1], cnt[:, t, :], AX.X, ALU.add).then_inc(S["rk"], 1)
                dve.wait_ge(S["rk"], 2 * t + 1)
                dve.scalar_tensor_tensor(out=mw[:, t:t + 1], in0=rank[:, t:t + 1], scalar=float(KK), in1=wt, op0=ALU.is_lt, op1=ALU.mult).then_inc(S["rk"], 1)
                dve.wait_ge(S["y"], t + 1)
                dve.tensor_tensor(yb[:, t % 2, :], ps[:, 4 + t % 2, 0:D], b2b[:, :], ALU.add).then_inc(S["yb"], 1)
                dve.wait_ge(S["yb"], t + 1)
                dve.wait_ge(S["rk"], 2 * t + 2)
                if t >= 4:
                    dve.wait_ge(s_out[t % 4], 16 * (t // 4))
                dve.scalar_tensor_tensor(out=ob[:, t % 4, :], in0=yb[:, t % 2, :], scalar=mw[:, t:t + 1], in1=x[:, t, :], op0=ALU.mult, op1=ALU.add).then_inc(S["fo"], 1)
                if t + BODY < NB:
                    to_xn(t + BODY)


_INS = ["x", "src", "dst", "edge_weight", "L0_gnn_W", "L0_gnn_a_src", "L0_gnn_a_dst", "L0_mix_W_qkv", "L0_mix_W_out",
        "L0_mix_b_out", "L0_ffn_wr", "L0_ffn_br", "L0_ffn_w1", "L0_ffn_b1", "L0_ffn_w2", "L0_ffn_b2"]


def kernel(**inputs):
    import concourse.bacc as _bacc
    from concourse.bass_utils import run_bass_kernel_spmd as _run

    nc = _bacc.Bacc("TRN2", target_bir_lowering=False, num_devices=1)
    arrays, args = {}, []
    for name in _INS:
        a = np.ascontiguousarray(inputs[name])
        arrays[f"in_{name}"] = a
        args.append(nc.dram_tensor(f"in_{name}", a.shape, mybir.dt.from_np(a.dtype), kind="ExternalInput").ap())
    out = nc.dram_tensor("out_0", inputs["x"].shape, F32, kind="ExternalOutput").ap()
    gps_layer(nc, *args, out)
    r = _run(nc, [arrays], core_ids=[0])
    return r.results[0]["out_0"]
```

```python
from contextlib import ExitStack

import numpy as np
import concourse.bass as bass
from concourse import mybir

P = 128
F32 = mybir.dt.float32
BF16 = mybir.dt.bfloat16
I32 = mybir.dt.int32
U16 = mybir.dt.uint16
ALU = mybir.AluOpType
ACT = mybir.ActivationFunctionType
AX = mybir.AxisListType

HEADS, OUT_F = 4, 64
MIX_HEADS, DIM_HEAD = 4, 32
NEG_SLOPE, LN_EPS, DEN_EPS = 0.2, 1e-5, 1e-10
LOWEST = -3.0e38
TILES = 4
RING = 4
LISTS = 8
BODY = 5


def gps_layer(nc, x_in, src_in, dst_in, ew_in, gw_in, gas_in, gad_in, wqkv_in, wout_in, bout_in,
              wr_in, br_in, w1_in, b1_in, w2_in, b2_in, out):
    N, D = x_in.shape
    E = src_in.shape[0]
    NB = -(-N // P)
    REST = N - (NB - 1) * P
    HF = HEADS * OUT_F
    ROW = HF + HEADS
    QK = MIX_HEADS * DIM_HEAD
    ADV = HEADS + QK
    HW = ROW + ADV
    FF = w1_in.shape[1]
    FC = FF // P
    KC = D // P
    GE = TILES * P
    NG = -(-E // GE)
    EREST = E - (NG - 1) * GE
    PAD = GE - EREST
    PREST = EREST // TILES
    LOOPS = NG // LISTS
    KSEL = max(1, int(0.5 * N))
    KK = KSEL - 1 if KSEL > 1 else 1
    assert EREST % TILES == 0 and D == HF == 256 and NB % BODY == 0 and QK == P

    htab = nc.dram_tensor("htab", (NB * P, ROW), F32, kind="Internal").ap()
    dstu_d = nc.dram_tensor("dstu_d", (NG, GE), U16, kind="Internal").ap()
    meta_d = nc.dram_tensor("meta_d", (NG, 2), I32, kind="Internal").ap()
    w_d = nc.dram_tensor("w_d", (NB, P), F32, kind="Internal").ap()

    with ExitStack() as ctx:
        def sb(name, shape, dt=F32):
            return ctx.enter_context(nc.sbuf_tensor(name, shape, dt))

        def sem(name):
            return ctx.enter_context(nc.semaphore(name))

        ps = ctx.enter_context(nc.psum_tensor("ps", [P, 8, 512], F32))

        x = sb("x", [P, NB, D])
        acc = sb("acc", [P, NB, ROW])
        kq = sb("kq", [P, 2, NB * P])
        adv = sb("adv", [P, NB, ADV])
        wbig = sb("wbig", [P, KC, HW])
        wqk = sb("wqk", [P, KC, 2 * QK])
        wout = sb("wout", [P, D])
        w1 = sb("w1", [P, KC, FF])
        w2 = sb("w2", [P, FC, D])
        b1 = sb("b1", [P, FC])
        b1r = sb("b1r", [FC, P])
        b2b = sb("b2b", [P, D])
        wrb = sb("wrb", [P, D])
        brb = sb("brb", [P, 1])
        boutb = sb("boutb", [P, D])
        avec = sb("avec", [P, 2, HF])
        stats = sb("stats", [P, BODY, 6])
        mv = sb("mv", [P, NB, 2])
        rstd = sb("rstd", [P, NB])
        sd = sb("sd", [P, NB])
        eps = sb("eps", [P, 1])
        xn = sb("xn", [P, BODY, D])
        xnT = sb("xnT", [P, BODY, KC, P])
        hst = sb("hst", [P, BODY, ROW])
        iota = sb("iota", [P, P])
        ident = sb("ident", [P, P])
        part = sb("part", [P, 1])
        tri = sb("tri", [P, P])
        nodeid = sb("nodeid", [P, NB])
        blkbase = sb("blkbase", [P, NB])
        ones = sb("ones", [1, P])
        zrow = sb("zrow", [1, 2 * P], BF16)
        zrow32 = sb("zrow32", [1, ROW])
        ad3 = sb("ad3", [P, NB, 3, HEADS], BF16)
        adr = sb("adr", [P, NB, 2, HEADS])
        dl = sb("dl", [NG, GE], I32)
        du = sb("du", [NG, GE], U16)
        mm = sb("mm", [NG, 2], I32)
        meta = sb("meta", [1, NG * 2], I32)
        srcr = sb("srcr", [P, LISTS, TILES], I32)
        wtr = sb("wtr", [P, LISTS, TILES])
        dcr = sb("dcr", [P, LISTS, TILES], I32)
        dlast = sb("dlast", [P, TILES], I32)
        dstb = sb("dstb", [P, LISTS, GE], U16)
        G = sb("G", [P, RING, TILES, ROW])
        free = G[:, :, :, :].rearrange("p q k c -> p (q k c)")
        aprod = free[:, 0:2 * KC * HF].rearrange("p (s c n) -> p s c n", s=2, c=KC)
        gsc = free[:, 0:BODY * D].rearrange("p (j n) -> p j n", j=BODY)
        yb = free[:, BODY * D:(BODY + 2) * D].rearrange("p (j n) -> p j n", j=2)
        ob = free[:, (BODY + 2) * D:(BODY + 6) * D].rearrange("p (j n) -> p j n", j=4)
        msg = sb("msg", [P, 2, TILES, ROW])
        oh = sb("oh", [P, 2, TILES, P])
        ohT = sb("ohT", [P, GE], BF16)
        et = sb("et", [P, 2, 17])
        rm = sb("rm", [P, 2])
        rg = sb("rg", [1, 2])
        rj = sb("rj", [1, P])
        Rsb = sb("Rsb", [P, 2])
        negR = sb("negR", [P, 2])
        Rlast = sb("Rlast", [P, NB])
        fsc = sb("fsc", [P, 2])
        Fin = sb("Fin", [P, NB])
        kmax = sb("kmax", [P, 2])
        ksum = sb("ksum", [P, 2])
        ekt = sb("ekt", [P, BODY, P])
        ctxT = sb("ctxT", [P, P])
        C2 = sb("C2", [P, D])
        rden = sb("rden", [P, 2, NB, HEADS])
        wtok = sb("wtok", [P, NB])
        wprod = sb("wprod", [P, D])
        wide = sb("wide", [P, NB * P])
        iotab = wide[:, :].rearrange("p (b n) -> p b n", b=NB)
        hT = wide[:, 0:2 * FC * P].rearrange("p (s c n) -> p s c n", s=2, c=FC)
        cnt = sb("cnt", [P, NB, 3])
        mw = sb("mw", [P, NB])
        rank = sb("rank", [P, NB])
        wrow = kq[:, 0, :]
        junk = kq[:, 1, :]
        wtT = sb("wtT", [NB, P])

        S = {}
        for name in ("const sp_go gp_go dve_go act_go sd ld_bo ld_w ld_bc ld_avec avs wbig st mv rstd xn tp xT h hst adv kqm kq xb "
                     "ld_dl dlp dlst meta ld_last ld_pad prep km ke ks ekT ek ctx ctxs c2 c2s mixm mix "
                     "e ec1 ec2 ec3 T rg B R nr ex msg agg0 ohTG ohTX adG adX ohG ohX aggG aggX accG accX fG fX finG finX iob "
                     "den gs x1 wt wtt wst wrow cnt rk x2 xn2 t2 x2T h1 g1 y yb fo acp accz "
                     ).split():
            S[name] = sem("s_" + name if not name.startswith("s_") else name)
        s_x = [sem(f"ld_x{i}") for i in range(NB // BODY)]
        s_tab = [sem(f"s_tab{i}") for i in range(BODY)]
        s_list = [sem(f"s_list{i}") for i in range(LISTS)]
        s_g = [sem(f"gathered{i}") for i in range(RING)]
        s_out = [sem(f"s_out{i}") for i in range(4)]

        block = ctx.enter_context(nc.Block())

        def groups(step):
            def run(eng):
                for q in range(LISTS):
                    step(q, q)
                with eng.Fori(1, LOOPS - 1):
                    for q in range(LISTS):
                        step(None, q)
                for g in range((LOOPS - 1) * LISTS, NG):
                    step(g, g % LISTS)
            return run

        numbers = iter(range(1000))

        def registers(eng, *values):
            made = []
            for v in values:
                made.append(eng.alloc_register(name=f"r{next(numbers)}"))
                eng.reg_mov(made[-1], v)
            return made

        def load_ranges(eng, regs, cursor, slot):
            eng.load([r for k in range(2) for r in regs[slot + k]], meta[0:1, bass.ds(eng.snap(cursor, min_val=0, max_val=NG // 2 - 1) * 4, 4)])
            eng.reg_add(cursor, cursor, 1)

        def blocks_of(eng, regs, slot):
            return tuple(eng.snap(r, min_val=0, max_val=NB - 1) for r in regs[slot])

        @block.sync
        def _(sp):
            with nc.allow_non_contiguous_dma(reason="weights, edge columns"):
                full = (NG - 1) * GE
                sp.dma_start(dl[0:NG - 1, :], dst_in[0:full].rearrange("(g j) -> g j", j=GE)).then_inc(S["ld_dl"], 16)
                sp.dma_start(dl[NG - 1:NG, 0:EREST], dst_in[full:E].rearrange("(g j) -> g j", g=1)).then_inc(S["ld_dl"], 16)
                sp.dma_start(dl[NG - 1:NG, EREST:GE], dst_in[E - PAD:E].rearrange("(g j) -> g j", g=1)).then_inc(S["ld_dl"], 16)
                for i in range(NB // BODY):
                    lo = i * BODY
                    if i < NB // BODY - 1:
                        sp.dma_start(x[:, lo:lo + BODY, :], x_in[lo * P:(lo + BODY) * P, :].rearrange("(b p) c -> p b c", p=P)).then_inc(s_x[i], 16)
                    else:
                        sp.dma_start(x[:, lo:NB - 1, :], x_in[lo * P:(NB - 1) * P, :].rearrange("(b p) c -> p b c", p=P)).then_inc(s_x[i], 16)
                        sp.wait_ge(S["const"], 1)
                        sp.dma_start(x[0:REST, NB - 1, :], x_in[(NB - 1) * P:N, :]).then_inc(s_x[i], 16)
                    if i == 0:
                        for kc in range(KC):
                            sp.dma_start(wbig[:, kc, 0:HF].rearrange("k (h o) -> k h o", h=HEADS),
                                         gw_in[:, kc * P:(kc + 1) * P, :].rearrange("h k o -> k h o")).then_inc(S["ld_w"], 16)
                            sp.dma_start(wbig[:, kc, HW - QK:HW], wqkv_in[kc * P:(kc + 1) * P, 2 * QK:3 * QK]).then_inc(S["ld_w"], 16)
                            sp.dma_start(wqk[:, kc, :], wqkv_in[kc * P:(kc + 1) * P, 0:2 * QK]).then_inc(S["ld_w"], 16)
                        sp.dma_start(avec[:, 0, :], gas_in.rearrange("(a h) o b -> a (h o b)", a=1).to_broadcast([P, HF])).then_inc(S["ld_avec"], 16)
                        sp.dma_start(avec[:, 1, :], gad_in.rearrange("(a h) o b -> a (h o b)", a=1).to_broadcast([P, HF])).then_inc(S["ld_avec"], 16)
                        sp.dma_start(boutb[:, :], bout_in.rearrange("(a d) -> a d", a=1).to_broadcast([P, D])).then_inc(S["ld_bo"], 16)
                sp.wait_ge(S["dlp"], 4)
                sp.dma_start(dstu_d[:, :], du[:, :]).then_inc(S["dlst"], 16)
                sp.dma_start(meta_d[:, :], mm[:, :]).then_inc(S["dlst"], 16)
                sp.wait_ge(S["dlst"], 32)
                sp.dma_start(meta[:, :], meta_d.rearrange("(a g) c -> a (g c)", a=1)).then_inc(S["meta"], 16)
                sp.wait_ge(S["const"], 2)
                sp.dma_start(dlast[0:PREST, :], dst_in[full:E].rearrange("(p k) -> p k", k=TILES)).then_inc(S["ld_last"], 16)
                for t in range(NB):
                    sp.wait_ge(S["hst"], t + 1)
                    sp.dma_start(htab[t * P:(t + 1) * P, :], hst[:, t % BODY, :]).then_inc(s_tab[t % BODY], 16)
                sp.dma_start(wout[:, :], wout_in).then_inc(S["ld_bc"], 16)
                sp.dma_start(w1[:, :, :], w1_in.rearrange("(c k) f -> k c f", k=P)).then_inc(S["ld_bc"], 16)
                sp.dma_start(w2[:, :, :], w2_in.rearrange("(c k) f -> k c f", k=P)).then_inc(S["ld_bc"], 16)
                sp.dma_start(b1r[:, :], b1_in.rearrange("(c k) -> c k", k=P)).then_inc(S["ld_bc"], 16)
                sp.dma_start(b2b[:, :], b2_in.rearrange("(a d) -> a d", a=1).to_broadcast([P, D])).then_inc(S["ld_bc"], 16)
                sp.dma_start(wrb[:, :], wr_in.rearrange("d (a b) -> a (d b)", a=1).to_broadcast([P, D])).then_inc(S["ld_bc"], 16)
                sp.dma_start(brb[:, :], br_in.rearrange("(a b) -> a b", a=1).to_broadcast([P, 1])).then_inc(S["ld_bc"], 16)

                m, row = registers(sp, 4, 0)

                def step(g, q):
                    if g is None or g >= LISTS:
                        sp.wait_ge(S["ohG"], m)
                        sp.sem_inc(S["sp_go"], 1)
                        sp.reg_add(m, m, 1)
                    r = sp.snap(row, min_val=0, max_val=NG - 2) if g is None else g
                    last = g == NG - 1
                    sp.dma_start(dstb[:, q, :], dstu_d[bass.ds(r, 1), :].to_broadcast([P, GE])).then_inc(s_list[q], 16)
                    for tile, array in ((srcr, src_in), (wtr, ew_in), (dcr, dst_in)):
                        if last:
                            sp.dma_start(tile[0:PREST, q, :], array[full:E].rearrange("(p k) -> p k", k=TILES)).then_inc(s_list[q], 16)
                            sp.dma_start(tile[PREST:P, q, :], array[E - PAD:E].rearrange("(p k) -> p k", k=TILES)).then_inc(S["ld_pad"], 16)
                        else:
                            sp.dma_start(tile[:, q, :], array[bass.ds(r * GE, GE)].rearrange("(p k) -> p k", k=TILES)).then_inc(s_list[q], 16)
                    sp.reg_add(row, row, 1)
                groups(step)(sp)

                sp.wait_ge(S["wtt"], 1)
                sp.dma_start(w_d[:, :], wtT[:, :]).then_inc(S["wst"], 16)
                sp.wait_ge(S["wst"], 16)
                sp.dma_start(wrow, w_d.rearrange("(a b) p -> a (b p)", a=1).to_broadcast([P, NB * P])).then_inc(S["wrow"], 16)
                for t in range(NB):
                    rows = P if t < NB - 1 else REST
                    sp.wait_ge(S["fo"], t + 1)
                    sp.dma_start(out[t * P:t * P + rows, :], ob[0:rows, t % 4, :]).then_inc(s_out[t % 4], 16)
                for k in range(4):
                    sp.wait_ge(s_out[k], 16 * len(range(k, NB, 4)))

        @block.gpsimd
        def _(gp):
            gp.memset(x[:, NB - 1, :], 0.0).then_inc(S["const"], 1)
            gp.memset(dlast[:, :], -1).then_inc(S["const"], 1)
            gp.iota(iota[:, :], [[1, P]], base=0, channel_multiplier=0, allow_small_or_imprecise_dtypes=True).then_inc(S["const"], 1)
            gp.iota(part[:, :], [[0, 1]], base=0, channel_multiplier=1, allow_small_or_imprecise_dtypes=True).then_inc(S["const"], 1)
            gp.iota(nodeid[:, :], [[P, NB]], base=0, channel_multiplier=1, allow_small_or_imprecise_dtypes=True).then_inc(S["const"], 1)
            gp.iota(blkbase[:, :], [[P, NB]], base=0, channel_multiplier=0, allow_small_or_imprecise_dtypes=True).then_inc(S["const"], 1)
            gp.memset(eps[:, :], LN_EPS).then_inc(S["const"], 1)
            gp.memset(ones[:, :], 1.0).then_inc(S["const"], 1)
            gp.memset(zrow[:, :], 0.0).then_inc(S["const"], 1)
            gp.memset(zrow32[:, :], 0.0).then_inc(S["const"], 1)
            gp.memset(et[:, :, :], LOWEST).then_inc(S["const"], 1)
            gp.memset(Rlast[:, :], LOWEST).then_inc(S["const"], 1)
            gp.memset(fsc[:, :], 0.0).then_inc(S["const"], 1)
            gp.memset(ctxT[:, :], 0.0).then_inc(S["const"], 1)
            gp.memset(acc[:, :, :], 0.0).then_inc(S["accz"], 1)
            for name, c in dict(adG=1, ec1=1, ec2=1, ec3=1, e=1, T=2, rg=2, ex=3, B=3, nr=3, msg=3, ohG=3,
                                aggG=4, fG=4, finG=4, accG=5, ohTX=1, adX=1, ohX=1, aggX=1, accX=1, fX=1, finX=1).items():
                gp.sem_inc(S[name], c)
            gp.wait_ge(S["ld_bo"], 16)
            for t in range(NB):
                gp.wait_ge(S["xn"], t + 1)
                gp.tensor_tensor(x[:, t, :], x[:, t, :], boutb[:, :], ALU.add).then_inc(S["xb"], 1)
            for j in range(BODY):
                gp.wait_ge(s_tab[j], 16 * (NB // BODY))

            n, lists = registers(gp, 4, 0)

            def step(g, q):
                if q == 0:
                    gp.reg_add(lists, lists, 16 * 4)
                if g == NG - 1:
                    gp.wait_ge(S["ld_pad"], 48)
                gp.wait_ge(s_list[q], lists)
                gp.sem_inc(S["gp_go"], 1)
                if g is None or g >= RING:
                    gp.wait_ge(S["msg"], n)
                    gp.sem_inc(S["gp_go"], 1)
                    gp.reg_add(n, n, 1)
                for k in range(TILES):
                    gp.indirect_dma_start(G[:, q % RING, k, :], None, htab, bass.IndirectOffsetOnAxis(ap=srcr[:, q, k:k + 1], axis=0)).then_inc(s_g[q % RING], 16)
            groups(step)(gp)

        @block.tensor
        def _(pe):
            pe.wait_ge(S["const"], 15)
            pe.wait_ge(S["ld_w"], 32 * 3)
            pe.wait_ge(S["wbig"], 1)

            def project(t):
                b = t % 2
                pe.wait_ge(S["xT"], t + 1)
                if t >= 2:
                    pe.wait_ge(S["adv"], t - 1)
                for kc in range(KC):
                    m = pe.matmul(ps[:, 2 + b, 0:HW], xnT[:, t % BODY, kc, :], wbig[:, kc, :], start=(kc == 0), stop=(kc == KC - 1))
                m.then_inc(S["h"], 1)
                if t >= 2:
                    pe.wait_ge(S["kq"], t - 1)
                for c in range(2):
                    for kc in range(KC):
                        m = pe.matmul(ps[:, 4 + b, c * P:(c + 1) * P], wqk[:, kc, (1 - c) * P:(2 - c) * P], xnT[:, t % BODY, kc, :],
                                      start=(kc == 0), stop=(kc == KC - 1))
                m.then_inc(S["kqm"], 1)

            for t in range(NB):
                pe.wait_ge(S["xn"], t + 1)
                if t >= 2:
                    pe.wait_ge(S["xT"], t - 1)
                for kc in range(KC):
                    m = pe.transpose(ps[:, t % 2, kc * P:(kc + 1) * P], xn[:, t % BODY, kc * P:(kc + 1) * P], ident[:, :])
                m.then_inc(S["tp"], 1)
                if t:
                    project(t - 1)
            project(NB - 1)

            for t in range(NB + 1):
                if t < NB:
                    if t == 0:
                        pe.wait_ge(S["ke"], 2)
                    if t >= 2:
                        pe.wait_ge(S["ek"], t - 1)
                    pe.transpose(ps[:, t % 2, 0:P], kq[:, 0, t * P:(t + 1) * P], ident[:, :]).then_inc(S["ekT"], 1)
                if t:
                    u = t - 1
                    pe.wait_ge(S["ek"], u + 1)
                    if u == 0:
                        pe.wait_ge(S["adv"], NB)
                    pe.matmul(ps[:, 6, 0:P], adv[:, u, HEADS:ADV], ekt[:, u % BODY, :], start=(u == 0), stop=(u == NB - 1)).then_inc(S["ctx"], 1)
            pe.wait_ge(S["ctxs"], MIX_HEADS)
            pe.wait_ge(S["ld_bc"], 16 * 7)
            pe.matmul(ps[:, 7, 0:D], ctxT[:, :], wout[:, :], start=True, stop=True).then_inc(S["c2"], 1)
            pe.wait_ge(S["c2s"], 1)
            for t in range(NB):
                if t >= 2:
                    pe.wait_ge(S["mix"], t - 1)
                pe.matmul(ps[:, 2 + t % 2, 0:D], kq[:, 1, t * P:(t + 1) * P], C2[:, :], start=True, stop=True).then_inc(S["mixm"], 1)
            pe.wait_ge(S["kq"], NB)
            pe.transpose(ps[:, 5, 0:FC], b1r[:, :], ident[0:FC, 0:FC]).then_inc(S["c2"], 1)

            pe.wait_ge(S["meta"], 16)
            pe.wait_ge(S["mix"], NB)
            pe.wait_ge(S["prep"], 1)
            pe.wait_ge(S["c2s"], 2)
            n, cursor, xa, xs, t = registers(pe, 4, 0, 1, 1, 0)
            regs = [registers(pe, 0, 0) for _ in range(LISTS)]

            def add_dst(p, b):
                for k in range(TILES):
                    for j in range(3):
                        m = pe.matmul(ps[:, p, 4 * k:4 * k + 4], ohT[:, k:GE:TILES], ad3[:, bass.ds(b, 1), j, :].rearrange("p a h -> p (a h)"),
                                      start=False, stop=False, skip_group_check=True)
                return m

            def expand(q, ready):
                if q % 2 == 0:
                    load_ranges(pe, regs, cursor, q)
                first, last = blocks_of(pe, regs, q)
                p = q % 2
                pe.matmul(ps[:, p, 0:16], zrow[:, 0:P], zrow[:, 0:16], start=True, stop=False, skip_group_check=True)
                with pe.If(first < last):
                    with pe.Fori(first, last) as b:
                        pe.reg_add(xa, xa, 1)
                        pe.wait_ge(S["ohTX"], xa)
                        add_dst(p, b).then_inc(S["adX"], 1)
                pe.wait_ge(S["ohTG"], ready)
                add_dst(p, last).then_inc(S["adG"], 1)

            def turn(q, ready):
                pe.wait_ge(S["e"], ready)
                pe.transpose(ps[0:1, 2, 0:P], rm[:, q % 2:q % 2 + 1], ident[:, :]).then_inc(S["T"], 1)

            def spread(q, ready):
                pe.wait_ge(S["rg"], ready)
                if ready is n:
                    pe.wait_ge(S["ex"], n)
                pe.matmul(ps[:, 5, 0:1], ones[:, :], rg[:, q % 2:q % 2 + 1], start=True, stop=True).then_inc(S["B"], 1)

            def add_messages(p, tiles=range(TILES)):
                for k in tiles:
                    m = pe.matmul(ps[:, 3 + p, 0:ROW], oh[:, p, k, :], msg[:, p, k, :], start=(k == 0), stop=(k == TILES - 1))
                return m

            def sums(q, between):
                first, last = blocks_of(pe, regs, q)
                p = q % 2
                pe.wait_ge(S["msg"], n)
                pe.wait_ge(S["accG"], n)
                with pe.If(first < last):
                    with pe.Fori(first, last) as b:
                        pe.wait_ge(S["accX"], xs)
                        pe.reg_add(xs, xs, 1)
                        pe.wait_ge(S["ohX"], xs)
                        add_messages(p).then_inc(S["aggX"], 1)
                pe.wait_ge(S["accX"], xs)
                pe.wait_ge(S["ohG"], n)
                add_messages(p, [0])
                between()
                add_messages(p, range(1, TILES)).then_inc(S["aggG"], 1)

            expand(0, 1)
            turn(0, 2)
            expand(1, 2)
            spread(0, 3)
            turn(1, 3)
            expand(2, 3)

            def step(g, q):
                sums(q, lambda: spread(q + 1, n) if g is None or g + 1 < NG else None)
                if g is None or g + 2 < NG:
                    turn(q + 2, n)
                if g is None or g + 3 < NG:
                    expand((q + 3) % LISTS, n)
                pe.reg_add(n, n, 1)
            groups(step)(pe)

            pe.wait_ge(S["wt"], NB)
            pe.transpose(ps[0:NB, 7, 0:P], wtok[:, :], ident[:, :]).then_inc(S["t2"], 1)

            def up(t):
                pe.wait_ge(S["x2T"], t + 1)
                if t >= 1:
                    pe.wait_ge(S["g1"], t)
                for c in range(FC):
                    for kc in range(KC):
                        m = pe.matmul(ps[:, 2 + c // 4, (c % 4) * P:(c % 4 + 1) * P], w1[:, kc, c * P:(c + 1) * P], xnT[:, t % BODY, kc, :],
                                      start=(kc == 0), stop=(kc == KC - 1))
                m.then_inc(S["h1"], 1)

            def down(t):
                pe.wait_ge(S["g1"], t + 1)
                if t >= 2:
                    pe.wait_ge(S["yb"], t - 1)
                for c in range(FC):
                    m = pe.matmul(ps[:, 4 + t % 2, 0:D], hT[:, t % 2, c, :], w2[:, c, :], start=(c == 0), stop=(c == FC - 1))
                m.then_inc(S["y"], 1)

            for t in range(NB + 1):
                if t < NB:
                    pe.wait_ge(S["xn2"], t + 1)
                    if t >= 2:
                        pe.wait_ge(S["x2T"], t - 1)
                    for kc in range(KC):
                        m = pe.transpose(ps[:, t % 2, kc * P:(kc + 1) * P], xn[:, t % BODY, kc * P:(kc + 1) * P], ident[:, :])
                    m.then_inc(S["t2"], 1)
                    up(t)
                if t:
                    down(t - 1)

        @block.scalar
        def _(act):
            act.wait_ge(S["const"], 15)

            def deviation(base, n, mvs):
                act.wait_ge(S["mv"], mvs)
                act.activation(sd[:, base:base + n], mv[:, base:base + n, 1:2].rearrange("p a b -> p (a b)"), ACT.Sqrt, bias=eps[:, 0:1]).then_inc(S["sd"], 1)

            def evacuate_kq(t):
                act.wait_ge(S["kqm"], t + 1)
                act.activation(kq[:, :, t * P:(t + 1) * P], ps[:, 4 + t % 2, 0:2 * P].rearrange("p (c n) -> p c n", c=2), ACT.Copy).then_inc(S["kq"], 1)

            deviation(0, BODY, BODY)
            for t in range(NB):
                if t % BODY == 2 and t + BODY < NB:
                    deviation(t - 2 + BODY, BODY, t - 2 + 2 * BODY)
                act.wait_ge(S["tp"], t + 1)
                if t >= BODY:
                    act.wait_ge(S["kqm"], t - BODY + 1)
                act.activation(xnT[:, t % BODY, :, :], ps[:, t % 2, 0:D].rearrange("p (c n) -> p c n", c=KC), ACT.Copy).then_inc(S["xT"], 1)
                if t:
                    evacuate_kq(t - 1)
            evacuate_kq(NB - 1)

            act.wait_ge(S["km"], 2)
            act.activation(kq[:, 0, 0:N], kq[:, 0, 0:N], ACT.Exp, bias=kmax[:, 1:2], accum_out=ksum[:, 0:1]).then_inc(S["ke"], 1)
            for t in range(NB):
                act.wait_ge(S["ekT"], t + 1)
                if t >= BODY:
                    act.wait_ge(S["ctx"], t - BODY + 1)
                act.activation(ekt[:, t % BODY, :], ps[:, t % 2, 0:P], ACT.Copy).then_inc(S["ek"], 1)
            act.wait_ge(S["c2"], 2)
            act.activation(b1[:, :], ps[:, 5, 0:FC], ACT.Copy).then_inc(S["c2s"], 1)

            act.wait_ge(S["meta"], 16)
            n, n3, n5, cursor, x_ = registers(act, 4, 3, 5, 0, 1)
            regs = [registers(act, 0, 0) for _ in range(LISTS)]

            def rescale(p, b, done, count, fdone):
                act.sem_inc(S["act_go"], 1)
                act.activation(fsc[:, p:p + 1], Rlast[:, bass.ds(b, 1)], ACT.Exp, bias=negR[:, p:p + 1]).then_inc(S[done], 1)
                act.wait_ge(S[done], count)
                act.sem_inc(S["act_go"], 1)
                act.activation(Rlast[:, bass.ds(b, 1)], Rsb[:, p:p + 1], ACT.Copy).then_inc(S[fdone], 1)

            def step(g, q):
                p = q % 2
                if q % 2 == 0:
                    load_ranges(act, regs, cursor, q)
                first, last = blocks_of(act, regs, q)
                act.wait_ge(S["B"], n)
                act.activation(negR[:, p:p + 1], ps[:, 5, 0:1], ACT.Copy, scale=-1.0).then_inc(S["nr"], 1)
                act.activation(Rsb[:, p:p + 1], ps[:, 5, 0:1], ACT.Copy).then_inc(S["nr"], 1)
                act.wait_ge(S["aggG"], n3)
                act.wait_ge(S["nr"], nr2)
                act.activation(msg[:, p, :, HF:ROW], et[:, p, 0:16].rearrange("p (k h) -> p k h", k=TILES), ACT.Exp, bias=negR[:, p:p + 1]).then_inc(S["ex"], 1)
                act.wait_ge(S["accG"], n)
                act.wait_ge(S["finG"], n)
                act.sem_inc(S["act_go"], 1)
                with act.If(first < last):
                    with act.Fori(first, last) as b:
                        act.wait_ge(S["accX"], x_)
                        act.wait_ge(S["finX"], x_)
                        act.reg_add(x_, x_, 1)
                        rescale(p, b, "fX", x_, "finX")
                act.wait_ge(S["accX"], x_)
                act.wait_ge(S["finX"], x_)
                rescale(p, last, "fG", n5, "finG")
                for r, by in ((n, 1), (n3, 1), (n5, 1), (nr2, 2)):
                    act.reg_add(r, r, by)
            nr2, = registers(act, 5)
            groups(step)(act)
            act.wait_ge(S["finG"], n)
            act.wait_ge(S["finX"], x_)
            act.activation(Fin[:, :], Rlast[:, :], ACT.Exp, bias=negR[:, (NG - 1) % 2:(NG - 1) % 2 + 1]).then_inc(S["den"], 1)

            deviation(0, NB, 2 * NB)
            act.wait_ge(S["t2"], 1)
            act.activation(wtT[:, :], ps[0:NB, 7, 0:P], ACT.Copy).then_inc(S["wtt"], 1)
            for t in range(NB):
                act.wait_ge(S["t2"], t + 2)
                if t >= BODY:
                    act.wait_ge(S["h1"], t - BODY + 1)
                act.activation(xnT[:, t % BODY, :, :], ps[:, t % 2, 0:D].rearrange("p (c n) -> p c n", c=KC), ACT.Copy).then_inc(S["x2T"], 1)
                act.wait_ge(S["h1"], t + 1)
                if t >= 2:
                    act.wait_ge(S["y"], t - 1)
                for c in range(FC):
                    m = act.activation(hT[:, t % 2, c, :], ps[:, 2 + c // 4, (c % 4) * P:(c % 4 + 1) * P], ACT.Gelu_apprx_tanh, bias=b1[:, c:c + 1])
                m.then_inc(S["g1"], 1)

        @block.vector
        def _(dve):
            dve.wait_ge(S["const"], 14)
            dve.tensor_scalar(ident[:, :], iota[:, :], part[:, 0:1], None, ALU.is_equal).then_inc(S["const"], 1)
            dve.tensor_scalar(tri[:, :], iota[:, :], part[:, 0:1], None, ALU.is_lt).then_inc(S["fo"], 0) if False else dve.tensor_scalar(tri[:, :], iota[:, :], part[:, 0:1], None, ALU.is_lt)
            dve.wait_ge(S["ld_dl"], 48)
            dve.tensor_copy(du[:, :], dl[:, :]).then_inc(S["dlp"], 1)
            dve.tensor_reduce(mm[:, 0:1], dl[:, :], AX.X, ALU.min).then_inc(S["dlp"], 1)
            dve.tensor_reduce(mm[:, 1:2], dl[:, :], AX.X, ALU.max).then_inc(S["dlp"], 1)
            dve.wait_ge(S["dlp"], 3)
            dve.tensor_scalar(mm[:, :], mm[:, :], 7, None, ALU.arith_shift_right).then_inc(S["dlp"], 1)
            dve.wait_ge(S["ld_avec"], 32)
            dve.wait_ge(S["ld_w"], 32 * 3)
            for s in range(2):
                dve.tensor_tensor(aprod[:, s, :, :], wbig[:, :, 0:HF], avec[:, s:s + 1, :].to_broadcast([P, KC, HF]), ALU.mult).then_inc(S["avs"], 1)
            dve.wait_ge(S["avs"], 2)
            for s in range(2):
                m = dve.tensor_reduce(wbig[:, :, HF + s * HEADS:HF + (s + 1) * HEADS], aprod[:, s, :, :].rearrange("p c (h o) -> p c h o", h=HEADS), AX.X, ALU.add)
            m.then_inc(S["wbig"], 1)

            def statistics(base, n, st0):
                for j in range(n):
                    dve.bn_stats(stats[:, j, :], x[:, base + j, :]).then_inc(S["st"], 1)
                dve.wait_ge(S["st"], st0 + n)
                for j in range(n):
                    dve.bn_aggr(mv[:, base + j, :], stats[:, j, :]).then_inc(S["mv"], 1)

            def invert(base, n, k):
                dve.wait_ge(S["sd"], k)
                dve.reciprocal(rstd[:, base:base + n], sd[:, base:base + n]).then_inc(S["rstd"], 1)
                dve.wait_ge(S["rstd"], k)

            def normed(t):
                return dve.tensor_scalar(xn[:, t % BODY, :], x[:, t, :], mv[:, t, 0:1], rstd[:, t:t + 1], ALU.subtract, ALU.mult)

            def evacuate_h(t):
                dve.wait_ge(S["h"], t + 1)
                if t >= BODY:
                    dve.wait_ge(s_tab[t % BODY], 16 * (t // BODY))
                dve.tensor_copy(hst[:, t % BODY, :], ps[:, 2 + t % 2, 0:ROW]).then_inc(S["hst"], 1)
                dve.tensor_copy(adv[:, t, :], ps[:, 2 + t % 2, ROW:HW]).then_inc(S["adv"], 1)

            for i in range(NB // BODY):
                dve.wait_ge(s_x[i], 16 if i < NB // BODY - 1 else 32)
                statistics(i * BODY, BODY, i * BODY)
                invert(i * BODY, BODY, i + 1)
                for j in range(BODY):
                    t = i * BODY + j
                    if t >= BODY:
                        dve.wait_ge(S["tp"], t - BODY + 1)
                    normed(t).then_inc(S["xn"], 1)
                    if t >= 3:
                        evacuate_h(t - 3)
            for t in range(NB - 3, NB):
                evacuate_h(t)

            dve.wait_ge(S["adv"], NB)
            dve.tensor_copy(ad3[:, :, 0, :], adv[:, :, 0:HEADS]).then_inc(S["acp"], 1)
            dve.wait_ge(S["acp"], 1)
            dve.tensor_tensor(adr[:, :, 0, :], adv[:, :, 0:HEADS], ad3[:, :, 0, :], ALU.subtract).then_inc(S["acp"], 1)
            dve.wait_ge(S["acp"], 2)
            dve.tensor_copy(ad3[:, :, 1, :], adr[:, :, 0, :]).then_inc(S["acp"], 1)
            dve.wait_ge(S["acp"], 3)
            dve.tensor_tensor(adr[:, :, 1, :], adr[:, :, 0, :], ad3[:, :, 1, :], ALU.subtract).then_inc(S["acp"], 1)
            dve.wait_ge(S["acp"], 4)
            dve.tensor_copy(ad3[:, :, 2, :], adr[:, :, 1, :]).then_inc(S["prep"], 1)

            dve.wait_ge(S["kq"], NB)
            dve.tensor_reduce(kmax[:, 0:1], kq[:, 0, 0:N], AX.X, ALU.max).then_inc(S["km"], 1)
            dve.wait_ge(S["km"], 1)
            dve.tensor_scalar(kmax[:, 1:2], kmax[:, 0:1], -1.0, None, ALU.mult).then_inc(S["km"], 1)
            dve.memset(kq[:, 0, N:NB * P], 0.0).then_inc(S["ke"], 1)
            dve.wait_ge(S["ke"], 2)
            dve.reciprocal(ksum[:, 1:2], ksum[:, 0:1]).then_inc(S["ks"], 1)
            dve.wait_ge(S["ctx"], NB)
            for h in range(MIX_HEADS):
                s = slice(h * DIM_HEAD, (h + 1) * DIM_HEAD)
                dve.tensor_copy(ctxT[s, s], ps[s, 6, s]).then_inc(S["ctxs"], 1)
            dve.wait_ge(S["c2"], 1)
            dve.wait_ge(S["ks"], 1)
            dve.tensor_scalar(C2[:, :], ps[:, 7, 0:D], ksum[:, 1:2], float(DIM_HEAD) ** -0.5, ALU.mult, ALU.mult).then_inc(S["c2s"], 1)
            dve.wait_ge(S["xb"], NB)
            for t in range(NB):
                dve.wait_ge(S["mixm"], t + 1)
                dve.tensor_tensor(x[:, t, :], ps[:, 2 + t % 2, 0:D], x[:, t, :], ALU.add).then_inc(S["mix"], 1)

            dve.wait_ge(S["meta"], 16)
            dve.wait_ge(S["accz"], 1)
            dve.tensor_tensor(iotab, iota[:, :].unsqueeze(1).to_broadcast([P, NB, P]), blkbase[:, :].unsqueeze(2).to_broadcast([P, NB, P]), ALU.add).then_inc(S["iob"], 1)
            dve.wait_ge(S["iob"], 1)
            n, cursor, lists, rows, xc, xv, t = registers(dve, 4, 0, 0, 0, 1, 1, 0)
            regs = [registers(dve, 0, 0) for _ in range(LISTS)]

            def columns(q, ready):
                if q % 2 == 0:
                    load_ranges(dve, regs, cursor, q)
                if q == 0:
                    dve.reg_add(lists, lists, 16 * 4)
                first, last = blocks_of(dve, regs, q)
                dve.wait_ge(s_list[q], lists)
                dve.wait_ge(S["adG"], ready)
                dve.sem_inc(S["dve_go"], 1)
                with dve.If(first < last):
                    with dve.Fori(first, last) as b:
                        dve.tensor_scalar(ohT[:, :], dstb[:, q, :], nodeid[:, bass.ds(b, 1)], None, ALU.is_equal).then_inc(S["ohTX"], 1)
                        dve.reg_add(xc, xc, 1)
                        dve.wait_ge(S["adX"], xc)
                        dve.sem_inc(S["dve_go"], 1)
                dve.tensor_scalar(ohT[:, :], dstb[:, q, :], nodeid[:, bass.ds(last, 1)], None, ALU.is_equal).then_inc(S["ohTG"], 1)

            def logits(q, ready, g=None):
                p = q % 2
                if q % RING == 0:
                    dve.reg_add(rows, rows, 16 * TILES)
                dve.wait_ge(s_g[q % RING], rows)
                if g == NG - 1:
                    dve.wait_ge(S["ld_pad"], 48)
                dve.wait_ge(S["adG"], ready)
                e16 = et[:, p, 0:16].rearrange("p (k h) -> p k h", k=TILES)
                dve.tensor_tensor(e16, ps[:, p, 0:16].rearrange("p (k h) -> p k h", k=TILES), G[:, q % RING, :, HF:ROW], ALU.add).then_inc(S["ec1"], 1)
                dve.wait_ge(S["ec1"], ready)
                dve.scalar_tensor_tensor(out=et[:, p, 0:16], in0=et[:, p, 0:16], scalar=NEG_SLOPE, in1=et[:, p, 0:16], op0=ALU.mult, op1=ALU.max).then_inc(S["ec2"], 1)
                dve.wait_ge(S["ec2"], ready)
                dve.tensor_tensor(e16, e16, wtr[:, q, :].unsqueeze(2).to_broadcast([P, TILES, HEADS]), ALU.mult).then_inc(S["ec3"], 1)
                dve.wait_ge(S["ec3"], ready)
                dve.tensor_reduce(rm[:, p:p + 1], et[:, p, 0:16], AX.X, ALU.max).then_inc(S["e"], 1)

            def group_max(q, ready):
                dve.wait_ge(S["T"], ready)
                before = LOWEST if ready == 3 else rg[:, (q + 1) % 2:(q + 1) % 2 + 1]
                dve.tensor_scalar(rj[:, :], ps[0:1, 2, 0:P], before, LOWEST, ALU.max, ALU.max, accum_out=rg[:, q % 2:q % 2 + 1]).then_inc(S["rg"], 1)

            def messages(q):
                p = q % 2
                dve.wait_ge(S["ex"], n)
                ex = msg[:, p, :, HF:ROW].unsqueeze(3).to_broadcast([P, TILES, HEADS, OUT_F])
                dve.tensor_tensor(msg[:, p, :, 0:HF].rearrange("p k (h o) -> p k h o", h=HEADS),
                                  G[:, q % RING, :, 0:HF].rearrange("p k (h o) -> p k h o", h=HEADS), ex, ALU.mult).then_inc(S["msg"], 1)

            def add_block(b, p, done):
                a = acc[:, bass.ds(b, 1), :].rearrange("p a c -> p (a c)")
                dve.scalar_tensor_tensor(out=a, in0=a, scalar=fsc[:, p:p + 1], in1=ps[:, 3 + p, 0:ROW], op0=ALU.mult, op1=ALU.add).then_inc(S[done], 1)

            def one_hot(g, q, b, done):
                d = dlast[:, :] if g == NG - 1 else dcr[:, q, :]
                dve.tensor_tensor(oh[:, q % 2, :, :], iotab[:, bass.ds(b, 1), :].to_broadcast([P, TILES, P]), d.unsqueeze(2).to_broadcast([P, TILES, P]), ALU.is_equal).then_inc(S[done], 1)

            def add_last(q):
                _, last = blocks_of(dve, regs, q)
                for name, r in (("aggG", n), ("fG", n), ("accG", n), ("accX", xv)):
                    dve.wait_ge(S[name], r)
                dve.sem_inc(S["dve_go"], 1)
                add_block(last, q % 2, "accG")

            def visit(g, q):
                first, last = blocks_of(dve, regs, q)
                with dve.If(first < last):
                    if g != 0:
                        add_last((q - 1) % LISTS)
                    dve.reg_add(t, n, 1)
                    if g != 0:
                        dve.wait_ge(S["accG"], t)
                        dve.sem_inc(S["dve_go"], 1)
                    with dve.Fori(first, last) as b:
                        one_hot(g, q, b, "ohX")
                        dve.wait_ge(S["accX"], xv)
                        dve.reg_add(xv, xv, 1)
                        dve.wait_ge(S["aggX"], xv)
                        dve.wait_ge(S["fX"], xv)
                        dve.sem_inc(S["dve_go"], 1)
                        add_block(b, q % 2, "accX")
                one_hot(g, q, last, "ohG")
                if g is None or g + 1 < NG:
                    group_max(q + 1, n)
                if g != 0:
                    with dve.If(last < first + 1):
                        add_last((q - 1) % LISTS)

            columns(0, 1)
            logits(0, 2)
            columns(1, 2)
            group_max(0, 3)
            logits(1, 3)
            columns(2, 3)

            def step(g, q):
                messages(q)
                visit(g, q)
                if g is None or g + 2 < NG:
                    logits((q + 2) % LISTS, n, g if g is None else g + 2)
                if g is None or g + 3 < NG:
                    columns((q + 3) % LISTS, n)
                dve.reg_add(n, n, 1)
            dve.wait_ge(S["ld_last"], 16)
            groups(step)(dve)
            add_last((NG - 1) % LISTS)
            dve.reg_add(n, n, 1)
            dve.wait_ge(S["accG"], n)
            dve.wait_ge(S["accX"], xv)

            dve.wait_ge(S["den"], 1)
            fb = Fin[:, :].unsqueeze(2).to_broadcast([P, NB, HEADS])
            dve.tensor_tensor(rden[:, 0, :, :], acc[:, 0:NB, HF:ROW], fb, ALU.mult).then_inc(S["gs"], 1)
            dve.wait_ge(S["gs"], 1)
            dve.tensor_scalar(rden[:, 1, :, :], rden[:, 0, :, :], DEN_EPS, None, ALU.add).then_inc(S["gs"], 1)
            dve.wait_ge(S["gs"], 2)
            dve.reciprocal(rden[:, 0, :, :], rden[:, 1, :, :]).then_inc(S["gs"], 1)
            dve.wait_ge(S["gs"], 3)
            dve.tensor_tensor(rden[:, 1, :, :], rden[:, 0, :, :], fb, ALU.mult).then_inc(S["gs"], 1)
            dve.wait_ge(S["gs"], 4)
            for i in range(NB // BODY):
                for j in range(BODY):
                    t = i * BODY + j
                    r = rden[:, 1, t, :].unsqueeze(2).to_broadcast([P, HEADS, OUT_F])
                    dve.tensor_tensor(gsc[:, j, :].rearrange("p (h o) -> p h o", h=HEADS), acc[:, t, 0:HF].rearrange("p (h o) -> p h o", h=HEADS), r, ALU.mult).then_inc(S["x1"], 1)
                dve.wait_ge(S["x1"], 2 * BODY * i + BODY)
                for j in range(BODY):
                    t = i * BODY + j
                    dve.tensor_tensor(x[:, t, :], x[:, t, :], gsc[:, j, :], ALU.add).then_inc(S["x1"], 1)
                dve.wait_ge(S["x1"], 2 * BODY * (i + 1))
                statistics(i * BODY, BODY, NB + i * BODY)
            invert(0, NB, NB // BODY + 1)
            for i in range(NB // BODY):
                for j in range(BODY):
                    t = i * BODY + j
                    xa = acc[:, t, 0:D]
                    dve.tensor_scalar(xa, x[:, t, :], mv[:, t, 0:1], rstd[:, t:t + 1], ALU.subtract, ALU.mult).then_inc(S["x2"], 1)
                dve.wait_ge(S["x2"], 2 * i * BODY + BODY)
                for j in range(BODY):
                    t = i * BODY + j
                    xa = acc[:, t, 0:D]
                    if t:
                        dve.wait_ge(S["wt"], t)
                    dve.tensor_tensor_reduce(wprod[:, :], xa, wrb[:, :], 1.0, brb[:, 0:1], ALU.mult, ALU.add, wtok[:, t:t + 1]).then_inc(S["wt"], 1)
                    dve.tensor_tensor(x[:, t, :], x[:, t, :], xa, ALU.add).then_inc(S["x2"], 1)

            def to_xn(t):
                if t >= BODY:
                    dve.wait_ge(S["t2"], t - BODY + 2)
                dve.tensor_copy(xn[:, t % BODY, :], acc[:, t, 0:D]).then_inc(S["xn2"], 1)

            for t in range(BODY):
                to_xn(t)
            dve.wait_ge(S["wrow"], 16)
            n = 0
            for t in range(NB):
                wt = wtok[:, t:t + 1]
                lo, hi = t * P, min((t + 1) * P, N)
                if t:
                    dve.wait_ge(S["cnt"], 3 * t)
                    dve.tensor_scalar(junk[:, 0:lo], wrow[:, 0:lo], wt, 0.0, ALU.is_ge, ALU.add, accum_out=cnt[:, t, 0:1]).then_inc(S["cnt"], 1)
                else:
                    dve.memset(cnt[:, t, 0:1], 0.0).then_inc(S["cnt"], 1)
                dve.tensor_scalar(junk[:, lo:N], wrow[:, lo:N], wt, 0.0, ALU.is_gt, ALU.add, accum_out=cnt[:, t, 1:2]).then_inc(S["cnt"], 1)
                dve.scalar_tensor_tensor(out=wprod[:, 0:hi - lo], in0=wrow[:, lo:hi], scalar=wt, in1=tri[:, 0:hi - lo], op0=ALU.is_equal, op1=ALU.mult, accum_out=cnt[:, t, 2:3]).then_inc(S["cnt"], 1)
                dve.wait_ge(S["cnt"], 3 * t + 3)
                dve.tensor_reduce(rank[:, t:t + 1], cnt[:, t, :], AX.X, ALU.add).then_inc(S["rk"], 1)
                dve.wait_ge(S["rk"], 2 * t + 1)
                dve.scalar_tensor_tensor(out=mw[:, t:t + 1], in0=rank[:, t:t + 1], scalar=float(KK), in1=wt, op0=ALU.is_lt, op1=ALU.mult).then_inc(S["rk"], 1)
                dve.wait_ge(S["y"], t + 1)
                dve.tensor_tensor(yb[:, t % 2, :], ps[:, 4 + t % 2, 0:D], b2b[:, :], ALU.add).then_inc(S["yb"], 1)
                dve.wait_ge(S["yb"], t + 1)
                dve.wait_ge(S["rk"], 2 * t + 2)
                if t >= 4:
                    dve.wait_ge(s_out[t % 4], 16 * (t // 4))
                dve.scalar_tensor_tensor(out=ob[:, t % 4, :], in0=yb[:, t % 2, :], scalar=mw[:, t:t + 1], in1=x[:, t, :], op0=ALU.mult, op1=ALU.add).then_inc(S["fo"], 1)
                if t + BODY < NB:
                    to_xn(t + BODY)


_INS = ["x", "src", "dst", "edge_weight", "L0_gnn_W", "L0_gnn_a_src", "L0_gnn_a_dst", "L0_mix_W_qkv", "L0_mix_W_out",
        "L0_mix_b_out", "L0_ffn_wr", "L0_ffn_br", "L0_ffn_w1", "L0_ffn_b1", "L0_ffn_w2", "L0_ffn_b2"]


def kernel(**inputs):
    import concourse.bacc as _bacc
    from concourse.bass_utils import run_bass_kernel_spmd as _run

    nc = _bacc.Bacc("TRN2", target_bir_lowering=False, num_devices=1)
    arrays, args = {}, []
    for name in _INS:
        a = np.ascontiguousarray(inputs[name])
        arrays[f"in_{name}"] = a
        args.append(nc.dram_tensor(f"in_{name}", a.shape, mybir.dt.from_np(a.dtype), kind="ExternalInput").ap())
    out = nc.dram_tensor("out_0", inputs["x"].shape, F32, kind="ExternalOutput").ap()
    gps_layer(nc, *args, out)
    r = _run(nc, [arrays], core_ids=[0])
    return r.results[0]["out_0"]
```

```python
from contextlib import ExitStack

import numpy as np
import concourse.bass as bass
from concourse import mybir

P = 128
F32 = mybir.dt.float32
BF16 = mybir.dt.bfloat16
I32 = mybir.dt.int32
U16 = mybir.dt.uint16
ALU = mybir.AluOpType
ACT = mybir.ActivationFunctionType
AX = mybir.AxisListType

HEADS, OUT_F = 4, 64
MIX_HEADS, DIM_HEAD = 4, 32
NEG_SLOPE, LN_EPS, DEN_EPS = 0.2, 1e-5, 1e-10
LOWEST = -3.0e38
TILES = 4
RING = 4
LISTS = 8
BODY = 5


def gps_layer(nc, x_in, src_in, dst_in, ew_in, gw_in, gas_in, gad_in, wqkv_in, wout_in, bout_in,
              wr_in, br_in, w1_in, b1_in, w2_in, b2_in, out):
    N, D = x_in.shape
    E = src_in.shape[0]
    NB = -(-N // P)
    REST = N - (NB - 1) * P
    HF = HEADS * OUT_F
    ROW = HF + HEADS
    QK = MIX_HEADS * DIM_HEAD
    ADV = HEADS + QK
    HW = ROW + ADV
    FF = w1_in.shape[1]
    FC = FF // P
    KC = D // P
    GE = TILES * P
    NG = -(-E // GE)
    EREST = E - (NG - 1) * GE
    PAD = GE - EREST
    PREST = EREST // TILES
    LOOPS = NG // LISTS
    KSEL = max(1, int(0.5 * N))
    KK = KSEL - 1 if KSEL > 1 else 1
    assert EREST % TILES == 0 and D == HF == 256 and NB % BODY == 0 and QK == P

    htab = nc.dram_tensor("htab", (NB * P, ROW), F32, kind="Internal").ap()
    dstu_d = nc.dram_tensor("dstu_d", (NG, GE), U16, kind="Internal").ap()
    dstm_d = nc.dram_tensor("dstm_d", (NG * GE,), I32, kind="Internal").ap()
    meta_d = nc.dram_tensor("meta_d", (NG, 3), I32, kind="Internal").ap()
    low_d = nc.dram_tensor("low_d", (NG, 1), I32, kind="Internal").ap()
    w_d = nc.dram_tensor("w_d", (NB, P), F32, kind="Internal").ap()

    with ExitStack() as ctx:
        def sb(name, shape, dt=F32):
            return ctx.enter_context(nc.sbuf_tensor(name, shape, dt))

        def sem(name):
            return ctx.enter_context(nc.semaphore(name))

        ps = ctx.enter_context(nc.psum_tensor("ps", [P, 8, 512], F32))

        x = sb("x", [P, NB, D])
        acc = sb("acc", [P, NB, ROW])
        kq = sb("kq", [P, 2, NB * P])
        adv = sb("adv", [P, NB, ADV])
        wbig = sb("wbig", [P, KC, HW])
        wqk = sb("wqk", [P, KC, 2 * QK])
        wout = sb("wout", [P, D])
        w1 = sb("w1", [P, KC, FF])
        w2 = sb("w2", [P, FC, D])
        b1 = sb("b1", [P, FC])
        b1r = sb("b1r", [FC, P])
        b2b = sb("b2b", [P, D])
        wrb = sb("wrb", [P, D])
        brb = sb("brb", [P, 1])
        boutb = sb("boutb", [P, D])
        avec = sb("avec", [P, 2, HF])
        stats = sb("stats", [P, BODY, 6])
        mv = sb("mv", [P, NB, 2])
        rstd = sb("rstd", [P, NB])
        sd = sb("sd", [P, NB])
        eps = sb("eps", [P, 1])
        xn = sb("xn", [P, BODY, D])
        xnT = sb("xnT", [P, BODY, KC, P])
        hst = sb("hst", [P, BODY, ROW])
        iota = sb("iota", [P, P])
        ident = sb("ident", [P, P])
        part = sb("part", [P, 1])
        tri = sb("tri", [P, P])
        nodeid = sb("nodeid", [P, NB])
        blkbase = sb("blkbase", [P, NB])
        ones = sb("ones", [1, P])
        zrow = sb("zrow", [1, 2 * P], BF16)
        ad3 = sb("ad3", [P, NB, 3, HEADS], BF16)
        adr = sb("adr", [P, NB, 2, HEADS])
        dl = sb("dl", [NG, GE], I32)
        du = sb("du", [NG, GE], U16)
        dn = sb("dn", [NG, 8], I32)
        mm = sb("mm", [NG, 3], I32)
        meta = sb("meta", [1, NG * 3], I32)
        neg1 = sb("neg1", [1, PAD], I32)
        low = sb("low", [P, NG], I32)
        mask = sb("mask", [P, 2, NG])
        srcr = sb("srcr", [P, LISTS, TILES], I32)
        wtr = sb("wtr", [P, LISTS, TILES])
        dcr = sb("dcr", [P, LISTS, TILES], I32)
        dmr = sb("dmr", [P, LISTS, TILES], I32)
        dlast = sb("dlast", [P, TILES], I32)
        dstb = sb("dstb", [P, LISTS, GE], U16)
        G = sb("G", [P, RING, TILES, ROW])
        free = G[:, :, :, :].rearrange("p q k c -> p (q k c)")
        aprod = free[:, 0:2 * KC * HF].rearrange("p (s c n) -> p s c n", s=2, c=KC)
        gsc = free[:, 0:BODY * D].rearrange("p (j n) -> p j n", j=BODY)
        ob = free[:, (BODY + 2) * D:(BODY + 6) * D].rearrange("p (j n) -> p j n", j=4)
        msg = sb("msg", [P, 2, TILES, ROW])
        oh = sb("oh", [P, 2, TILES, P])
        ohT = sb("ohT", [P, 2, GE], BF16)
        et = sb("et", [P, 2, 17])
        rm = sb("rm", [P, 2])
        rg = sb("rg", [1, 2])
        rj = sb("rj", [1, P])
        Rsb = sb("Rsb", [P, 2])
        negR = sb("negR", [P, 2])
        Rlast = sb("Rlast", [P, NB])
        fsc = sb("fsc", [P, 2])
        fscM = sb("fscM", [P, 2])
        Fin = sb("Fin", [P, NB])
        kmax = sb("kmax", [P, 2])
        ksum = sb("ksum", [P, 2])
        ksums = sb("ksums", [P, NB // BODY])
        kmaxs = sb("kmaxs", [P, NB // BODY])
        ekt = sb("ekt", [P, BODY, P])
        ctxT = sb("ctxT", [P, P])
        C2 = sb("C2", [P, D])
        rden = sb("rden", [P, 2, NB, HEADS])
        wtok = sb("wtok", [P, NB])
        wprod = sb("wprod", [P, D])
        wide = sb("wide", [P, NB * P])
        dm = wide[0:NG, 0:GE].bitcast(I32)
        parts = hst[:, 0:2, :]
        iotab = wide[:, :].rearrange("p (b n) -> p b n", b=NB)
        hT = wide[:, 0:2 * FC * P].rearrange("p (s c n) -> p s c n", s=2, c=FC)
        cnt = sb("cnt", [P, NB, 3])
        mw = sb("mw", [P, NB])
        rank = sb("rank", [P, NB])
        wrow = kq[:, 0, :]
        junk = kq[:, 1, :]
        wtT = sb("wtT", [NB, P])

        S = {}
        for name in ("constants_ready y_weighted gelu_table masks_ready k_padding_zero wqkv_loaded "
                     "block_iota_ready kmax_of_batch sp_go gp_go dve_go act_go deviation_ready b_out_loaded "
                     "w_loaded late_weights_loaded a_loaded w_times_a w_a_ready stats_ready mean_var_ready "
                     "rstd_ready xn_ready xn_turned xnT_ready h_projected rows_staged attn_dst_v_taken "
                     "kq_projected kq_taken b_out_added dst_loaded table_steps tables_stored ranges_loaded "
                     "last_dst_loaded padding_loaded attn_dst_split kmax_steps k_exp ksum_steps ek_turned "
                     "ek_taken context_summed context_taken c2_multiplied c2_taken mix_multiplied mix_added "
                     "edge_max logit_sum logit_leaky logit_weighted max_turned running_max max_spread "
                     "max_copied exp_ready messages_ready columns_last columns_block attn_dst_last "
                     "attn_dst_block onehot_last onehot_block summed_last summed_block added_last added_block "
                     "added_first sums_split factor_last factor_block factor_first max_kept_first "
                     "max_kept_last max_kept_block final_factors denominator_steps x1_steps weight_ready "
                     "weights_turned weights_taken weights_stored weights_spread counted rank_steps xn2_added "
                     "xn2_ready xn2_turned xn2T_ready hidden_ready gelu_ready y_ready y_taken out_staged "
                     "split_steps acc_zeroed").split():
            S[name] = sem("s_" + name)
        s_x = [sem(f"ld_x{i}") for i in range(NB // BODY)]
        s_tab = [sem(f"s_tab{i}") for i in range(BODY)]
        s_list = [sem(f"s_list{i}") for i in range(LISTS)]
        s_g = [sem(f"gathered{i}") for i in range(RING)]
        s_out = [sem(f"s_out{i}") for i in range(4)]

        FIRST_BATCHES = ((0, 1), (1, BODY - 1))
        TURN_BANKS, MIX_BANKS = (3, 4, 6), (3, 4, 6, 7)
        WT_AT = 6
        DLP = 12

        block = ctx.enter_context(nc.Block())

        def groups(step, peeled=True):
            def run(eng):
                for q in range(LISTS if peeled else 0):
                    step(q, q)
                with eng.Fori(1, LOOPS - 1):
                    for q in range(LISTS):
                        step(None, q)
                for g in range((LOOPS - 1) * LISTS, NG):
                    step(g, g % LISTS)
            return run

        numbers = iter(range(1000))

        def registers(eng, *values):
            made = []
            for v in values:
                made.append(eng.alloc_register(name=f"r{next(numbers)}"))
                eng.reg_mov(made[-1], v)
            return made

        def load_ranges(eng, regs, cursor, slot):
            eng.load([r for k in range(2) for r in regs[slot + k]], meta[0:1, bass.ds(eng.snap(cursor, min_val=0, max_val=NG // 2 - 1) * 6, 6)])
            eng.reg_add(cursor, cursor, 1)

        def blocks_of(eng, regs, slot):
            return tuple(eng.snap(r, min_val=0, max_val=NB - 1) for r in regs[slot])

        @block.sync
        def _(sp):
            with nc.allow_non_contiguous_dma(reason="weights, edge columns"):
                full = (NG - 1) * GE

                def load_tokens(i):
                    lo = i * BODY
                    if i < NB // BODY - 1:
                        sp.dma_start(x[:, lo:lo + BODY, :], x_in[lo * P:(lo + BODY) * P, :].rearrange("(b p) c -> p b c", p=P)).then_inc(s_x[i], 16)
                    else:
                        sp.dma_start(x[:, lo:NB - 1, :], x_in[lo * P:(NB - 1) * P, :].rearrange("(b p) c -> p b c", p=P)).then_inc(s_x[i], 16)
                        sp.wait_ge(S["constants_ready"], 1)
                        sp.dma_start(x[0:REST, NB - 1, :], x_in[(NB - 1) * P:N, :]).then_inc(s_x[i], 16)

                load_tokens(0)
                for kc in range(KC):
                    sp.dma_start(wbig[:, kc, 0:HF].rearrange("k (h o) -> k h o", h=HEADS),
                                 gw_in[:, kc * P:(kc + 1) * P, :].rearrange("h k o -> k h o")).then_inc(S["w_loaded"], 16)
                for which, array in enumerate((gas_in, gad_in)):
                    sp.dma_start(avec[:, which, :], array.rearrange("(a h) o b -> a (h o b)", a=1).to_broadcast([P, HF])).then_inc(S["a_loaded"], 16)
                for kc in range(KC):
                    sp.dma_start(wbig[:, kc, HW - QK:HW], wqkv_in[kc * P:(kc + 1) * P, 2 * QK:3 * QK]).then_inc(S["wqkv_loaded"], 16)
                    sp.dma_start(wqk[:, kc, :], wqkv_in[kc * P:(kc + 1) * P, 0:2 * QK]).then_inc(S["wqkv_loaded"], 16)
                load_tokens(1)
                sp.dma_start(boutb[:, :], bout_in.rearrange("(a d) -> a d", a=1).to_broadcast([P, D])).then_inc(S["b_out_loaded"], 16)
                sp.dma_start(dl[0:NG - 1, :], dst_in[0:full].rearrange("(g j) -> g j", j=GE)).then_inc(S["dst_loaded"], 16)
                sp.dma_start(dl[NG - 1:NG, 0:EREST], dst_in[full:E].rearrange("(g j) -> g j", g=1)).then_inc(S["dst_loaded"], 16)
                sp.dma_start(dl[NG - 1:NG, EREST:GE], dst_in[E - PAD:E].rearrange("(g j) -> g j", g=1)).then_inc(S["dst_loaded"], 16)
                for i in range(2, NB // BODY):
                    load_tokens(i)
                sp.wait_ge(S["table_steps"], DLP)
                sp.dma_start(dstu_d[:, :], du[:, :]).then_inc(S["tables_stored"], 16)
                sp.dma_start(meta_d[:, :], mm[:, :]).then_inc(S["tables_stored"], 16)
                sp.dma_start(low_d[:, :], dn[:, 6:7]).then_inc(S["tables_stored"], 16)
                sp.dma_start(dstm_d.rearrange("(g j) -> g j", j=GE), dm).then_inc(S["tables_stored"], 16)
                sp.wait_ge(S["constants_ready"], 3)
                sp.wait_ge(S["tables_stored"], 64)
                sp.dma_start(dstm_d[E:NG * GE].rearrange("(a j) -> a j", a=1), neg1[:, :]).then_inc(S["tables_stored"], 16)
                sp.dma_start(meta[:, :], meta_d.rearrange("(a g) c -> a (g c)", a=1)).then_inc(S["ranges_loaded"], 16)
                sp.dma_start(low[:, :], low_d.rearrange("(a g) c -> a (g c)", a=1).to_broadcast([P, NG])).then_inc(S["ranges_loaded"], 16)
                sp.wait_ge(S["tables_stored"], 80)
                sp.dma_start(dlast[0:PREST, :], dst_in[full:E].rearrange("(p k) -> p k", k=TILES)).then_inc(S["last_dst_loaded"], 16)

                def store_rows(t):
                    sp.wait_ge(S["rows_staged"], t + 1)
                    sp.dma_start(htab[t * P:(t + 1) * P, :], hst[:, t % BODY, :]).then_inc(s_tab[t % BODY], 16)

                m, row = registers(sp, 4, 0)

                def step(g, q):
                    if g is None or g >= LISTS:
                        sp.wait_ge(S["onehot_last"], m)
                        sp.sem_inc(S["sp_go"], 1)
                        sp.reg_add(m, m, 1)
                    r = sp.snap(row, min_val=0, max_val=NG - 2) if g is None else g
                    last = g == NG - 1
                    sp.dma_start(dstb[:, q, :], dstu_d[bass.ds(r, 1), :].to_broadcast([P, GE])).then_inc(s_list[q], 16)
                    sp.dma_start(dmr[:, q, :], dstm_d[bass.ds(r * GE, GE)].rearrange("(p k) -> p k", k=TILES)).then_inc(s_list[q], 16)
                    for tile, array in ((srcr, src_in), (wtr, ew_in), (dcr, dst_in)):
                        if last:
                            sp.dma_start(tile[0:PREST, q, :], array[full:E].rearrange("(p k) -> p k", k=TILES)).then_inc(s_list[q], 16)
                            sp.dma_start(tile[PREST:P, q, :], array[E - PAD:E].rearrange("(p k) -> p k", k=TILES)).then_inc(S["padding_loaded"], 16)
                        else:
                            sp.dma_start(tile[:, q, :], array[bass.ds(r * GE, GE)].rearrange("(p k) -> p k", k=TILES)).then_inc(s_list[q], 16)
                    sp.reg_add(row, row, 1)
                loads = [(wout[:, :], wout_in),
                         (b2b[:, :], b2_in.rearrange("(a d) -> a d", a=1).to_broadcast([P, D])),
                         (wrb[:, :], wr_in.rearrange("d (a b) -> a (d b)", a=1).to_broadcast([P, D])),
                         (brb[:, :], br_in.rearrange("(a b) -> a b", a=1).to_broadcast([P, 1])),
                         (b1r[:, :], b1_in.rearrange("(c k) -> c k", k=P))]
                loads += [(w1[:, c, :], w1_in[c * P:(c + 1) * P, :]) for c in range(KC)]
                loads += [(w2[:, c:c + 4, :], w2_in[c * P:(c + 4) * P, :].rearrange("(c k) f -> k c f", k=P)) for c in range(0, FC, 4)]
                for t in range(NB):
                    store_rows(t)
                    if 2 <= t < 2 + len(loads):
                        sp.dma_start(loads[t - 2][0], loads[t - 2][1]).then_inc(S["late_weights_loaded"], 16)
                    if NB - LISTS - 2 <= t < NB - 2:
                        step(t - (NB - LISTS - 2), t - (NB - LISTS - 2))
                groups(step, peeled=False)(sp)

                sp.wait_ge(S["weights_taken"], 1)
                sp.dma_start(w_d[:, :], wtT[:, :]).then_inc(S["weights_stored"], 16)
                sp.wait_ge(S["weights_stored"], 16)
                sp.dma_start(wrow, w_d.rearrange("(a b) p -> a (b p)", a=1).to_broadcast([P, NB * P])).then_inc(S["weights_spread"], 16)
                for t in range(NB):
                    rows = P if t < NB - 1 else REST
                    sp.wait_ge(S["out_staged"], t + 1)
                    sp.dma_start(out[t * P:t * P + rows, :], ob[0:rows, t % 4, :]).then_inc(s_out[t % 4], 16)
                for k in range(4):
                    sp.wait_ge(s_out[k], 16 * len(range(k, NB, 4)))

        @block.gpsimd
        def _(gp):
            gp.memset(x[:, NB - 1, :], 0.0).then_inc(S["constants_ready"], 1)
            gp.memset(dlast[:, :], -1).then_inc(S["constants_ready"], 1)
            gp.memset(neg1[:, :], -1).then_inc(S["constants_ready"], 1)
            gp.iota(iota[:, :], [[1, P]], base=0, channel_multiplier=0, allow_small_or_imprecise_dtypes=True).then_inc(S["constants_ready"], 1)
            gp.iota(part[:, :], [[0, 1]], base=0, channel_multiplier=1, allow_small_or_imprecise_dtypes=True).then_inc(S["constants_ready"], 1)
            gp.iota(nodeid[:, :], [[P, NB]], base=0, channel_multiplier=1, allow_small_or_imprecise_dtypes=True).then_inc(S["constants_ready"], 1)
            gp.iota(blkbase[:, :], [[P, NB]], base=0, channel_multiplier=0, allow_small_or_imprecise_dtypes=True).then_inc(S["constants_ready"], 1)
            gp.memset(eps[:, :], LN_EPS).then_inc(S["constants_ready"], 1)
            gp.memset(ones[:, :], 1.0).then_inc(S["constants_ready"], 1)
            gp.memset(zrow[:, :], 0.0).then_inc(S["constants_ready"], 1)
            gp.memset(et[:, :, :], LOWEST).then_inc(S["constants_ready"], 1)
            gp.memset(Rlast[:, :], LOWEST).then_inc(S["constants_ready"], 1)
            gp.memset(fsc[:, :], 0.0).then_inc(S["constants_ready"], 1)
            gp.memset(ctxT[:, :], 0.0).then_inc(S["constants_ready"], 1)
            gp.memset(acc[:, :, :], 0.0).then_inc(S["acc_zeroed"], 1)
            for name, c in dict(attn_dst_last=1, logit_sum=1, logit_leaky=1, logit_weighted=1, edge_max=1, max_turned=2, running_max=2,
                                exp_ready=3, max_spread=3, max_copied=3, messages_ready=3, onehot_last=3, summed_last=4, factor_last=4,
                                max_kept_last=4, added_last=5, columns_block=1, attn_dst_block=1, onehot_block=1, summed_block=1,
                                added_block=1, factor_block=1, max_kept_block=1, added_first=1, factor_first=1, max_kept_first=1,
                                sums_split=2).items():
                gp.sem_inc(S[name], c)
            gp.wait_ge(S["b_out_loaded"], 16)
            for t in range(NB):
                if t == NB - BODY:
                    gp.wait_ge(S["tables_stored"], 80)
                    gp.tensor_tensor(iotab, iota[:, :].unsqueeze(1).to_broadcast([P, NB, P]), blkbase[:, :].unsqueeze(2).to_broadcast([P, NB, P]), ALU.add).then_inc(S["block_iota_ready"], 1)
                gp.wait_ge(S["xn_ready"], t + 1)
                gp.tensor_tensor(x[:, t, :], x[:, t, :], boutb[:, :], ALU.add).then_inc(S["b_out_added"], 1)
            for j in range(BODY):
                gp.wait_ge(s_tab[j], 16 * (NB // BODY))

            n, lists = registers(gp, 4, 0)

            def step(g, q):
                if q == 0:
                    gp.reg_add(lists, lists, 16 * 5)
                if g == NG - 1:
                    gp.wait_ge(S["padding_loaded"], 48)
                gp.wait_ge(s_list[q], lists)
                gp.sem_inc(S["gp_go"], 1)
                if g is None or g >= RING:
                    gp.wait_ge(S["messages_ready"], n)
                    gp.sem_inc(S["gp_go"], 1)
                    gp.reg_add(n, n, 1)
                for k in range(TILES):
                    gp.indirect_dma_start(G[:, q % RING, k, :], None, htab, bass.IndirectOffsetOnAxis(ap=srcr[:, q, k:k + 1], axis=0)).then_inc(s_g[q % RING], 16)
            groups(step)(gp)

            for t in range(NB):
                gp.wait_ge(S["xn2_ready"], t + 1)
                gp.tensor_tensor(x[:, t, :], x[:, t, :], acc[:, t, 0:D], ALU.add).then_inc(S["xn2_added"], 1)
            for t in range(NB):
                gp.wait_ge(S["y_taken"], t + 1)
                gp.wait_ge(S["xn2_added"], t + 1)
                gp.wait_ge(S["rank_steps"], 2 * t + 2)
                if t >= 4:
                    gp.wait_ge(s_out[t % 4], 16 * (t // 4))
                gp.tensor_scalar(ob[:, t % 4, :], acc[:, t, 0:D], mw[:, t:t + 1], None, ALU.mult).then_inc(S["y_weighted"], 1)
                gp.wait_ge(S["y_weighted"], t + 1)
                gp.tensor_tensor(ob[:, t % 4, :], ob[:, t % 4, :], x[:, t, :], ALU.add).then_inc(S["out_staged"], 1)

        @block.tensor
        def _(pe):
            pe.wait_ge(S["constants_ready"], 15)

            def project(t):
                b = t % 2
                if t == 0:
                    pe.wait_ge(S["w_loaded"], 32)
                    pe.wait_ge(S["wqkv_loaded"], 64)
                    pe.wait_ge(S["w_a_ready"], 1)
                pe.wait_ge(S["xnT_ready"], t + 1)
                if t >= 2:
                    pe.wait_ge(S["attn_dst_v_taken"], t - 1)
                for kc in range(KC):
                    m = pe.matmul(ps[:, 2 + b, 0:HW], xnT[:, t % BODY, kc, :], wbig[:, kc, :], start=(kc == 0), stop=(kc == KC - 1))
                m.then_inc(S["h_projected"], 1)
                if t >= 2:
                    pe.wait_ge(S["kq_taken"], t - 1)
                for c in range(2):
                    for kc in range(KC):
                        m = pe.matmul(ps[:, 4 + b, c * P:(c + 1) * P], wqk[:, kc, (1 - c) * P:(2 - c) * P], xnT[:, t % BODY, kc, :],
                                      start=(kc == 0), stop=(kc == KC - 1))
                m.then_inc(S["kq_projected"], 1)

            for t in range(NB):
                pe.wait_ge(S["xn_ready"], t + 1)
                if t >= 2:
                    pe.wait_ge(S["xnT_ready"], t - 1)
                for kc in range(KC):
                    m = pe.transpose(ps[:, t % 2, kc * P:(kc + 1) * P], xn[:, t % BODY, kc * P:(kc + 1) * P], ident[:, :])
                m.then_inc(S["xn_turned"], 1)
                if t:
                    project(t - 1)
            project(NB - 1)

            pe.wait_ge(S["ranges_loaded"], 32)
            pe.wait_ge(S["attn_dst_split"], 1)
            pe.wait_ge(S["xnT_ready"], NB)
            pe.wait_ge(S["attn_dst_v_taken"], NB)
            pe.wait_ge(S["kq_taken"], NB)
            n, cursor, expanded, visited = registers(pe, 4, 0, 1, 1)
            regs = [registers(pe, 0, 0, 0) for _ in range(LISTS)]

            def add_dst(p, b, columns):
                for k in range(TILES):
                    for j in range(3):
                        m = pe.matmul(ps[:, p, 4 * k:4 * k + 4], ohT[:, columns, k:GE:TILES], ad3[:, bass.ds(b, 1), j, :].rearrange("p a h -> p (a h)"),
                                      start=False, stop=False, skip_group_check=True)
                return m

            def expand(q, ready):
                first, _, last = blocks_of(pe, regs, q)
                p = q % 2
                pe.matmul(ps[:, p, 0:16], zrow[:, 0:P], zrow[:, 0:16], start=True, stop=False, skip_group_check=True)
                with pe.If(first < last):
                    with pe.Fori(first, last) as b:
                        pe.reg_add(expanded, expanded, 1)
                        pe.wait_ge(S["columns_block"], expanded)
                        add_dst(p, b, 1).then_inc(S["attn_dst_block"], 1)
                pe.wait_ge(S["columns_last"], ready)
                add_dst(p, last, 0).then_inc(S["attn_dst_last"], 1)

            def turn(q, ready):
                pe.wait_ge(S["edge_max"], ready)
                pe.transpose(ps[0:1, 2, 0:P], rm[:, q % 2:q % 2 + 1], ident[:, :]).then_inc(S["max_turned"], 1)

            def spread(q, ready):
                pe.wait_ge(S["running_max"], ready)
                if ready is n:
                    pe.wait_ge(S["exp_ready"], n)
                pe.matmul(ps[:, 5, 0:1], ones[:, :], rg[:, q % 2:q % 2 + 1], start=True, stop=True).then_inc(S["max_spread"], 1)

            def add_messages(p, tiles=range(TILES)):
                for k in tiles:
                    m = pe.matmul(ps[:, 3 + p, 0:ROW], oh[:, p, k, :], msg[:, p, k, :], start=(k == 0), stop=(k == TILES - 1))
                return m

            def sums(q, between):
                _, start, last = blocks_of(pe, regs, q)
                p = q % 2
                pe.wait_ge(S["messages_ready"], n)
                pe.wait_ge(S["added_last"], n)
                with pe.If(start < last):
                    with pe.Fori(start, last) as b:
                        pe.wait_ge(S["added_block"], visited)
                        pe.reg_add(visited, visited, 1)
                        pe.wait_ge(S["onehot_block"], visited)
                        add_messages(p).then_inc(S["summed_block"], 1)
                pe.wait_ge(S["added_block"], visited)
                pe.wait_ge(S["onehot_last"], n)
                add_messages(p, [0])
                between()
                add_messages(p, range(1, TILES)).then_inc(S["summed_last"], 1)

            load_ranges(pe, regs, cursor, 0)
            load_ranges(pe, regs, cursor, 2)
            expand(0, 1)
            for t in range(NB + 2):
                if t == 12:
                    expand(1, 2)
                if t == 20:
                    turn(0, 2)
                if t < NB:
                    pe.wait_ge(S["k_exp"], 1 + t // BODY)
                    if t == NB - 1:
                        pe.wait_ge(S["k_padding_zero"], 1)
                    if t >= 3:
                        pe.wait_ge(S["ek_taken"], t - 2)
                    pe.transpose(ps[:, TURN_BANKS[t % 3], 0:P], kq[:, 0, t * P:(t + 1) * P], ident[:, :]).then_inc(S["ek_turned"], 1)
                if t >= 2:
                    u = t - 2
                    pe.wait_ge(S["ek_taken"], u + 1)
                    pe.matmul(ps[:, 7, 0:P], adv[:, u, HEADS:ADV], ekt[:, u % BODY, :], start=(u == 0), stop=(u == NB - 1)).then_inc(S["context_summed"], 1)
            spread(0, 3)
            turn(1, 3)
            expand(2, 3)
            pe.wait_ge(S["context_taken"], MIX_HEADS)
            pe.wait_ge(S["late_weights_loaded"], 16 * 9)
            pe.matmul(ps[:, 6, 0:D], ctxT[:, :], wout[:, :], start=True, stop=True).then_inc(S["c2_multiplied"], 1)
            pe.wait_ge(S["c2_taken"], 1)
            for t in range(NB):
                if t >= 4:
                    pe.wait_ge(S["mix_added"], t - 3)
                pe.matmul(ps[:, MIX_BANKS[t % 4], 0:D], kq[:, 1, t * P:(t + 1) * P], C2[:, :], start=True, stop=True).then_inc(S["mix_multiplied"], 1)
            pe.wait_ge(S["mix_added"], NB)

            def step(g, q):
                sums(q, lambda: spread(q + 1, n) if g is None or g + 1 < NG else None)
                if q % 2 == 1 and (g is None or g + 3 < NG):
                    load_ranges(pe, regs, cursor, (q + 3) % LISTS)
                if g is None or g + 2 < NG:
                    turn(q + 2, n)
                if g is None or g + 3 < NG:
                    expand((q + 3) % LISTS, n)
                pe.reg_add(n, n, 1)
            groups(step)(pe)

            def turn_tokens(t):
                pe.wait_ge(S["xn2_ready"], t + 1)
                if t >= 2:
                    pe.wait_ge(S["xn2T_ready"], t - 1)
                for kc in range(KC):
                    m = pe.transpose(ps[:, t % 2, kc * P:(kc + 1) * P], acc[:, t, kc * P:(kc + 1) * P], ident[:, :])
                m.then_inc(S["xn2_turned"], 1)

            def up(t):
                pe.wait_ge(S["xn2T_ready"], t + 1)
                for half in range(2):
                    if t >= 1:
                        pe.wait_ge(S["gelu_ready"], 2 * t - 1 + half)
                    for c in range(half * FC // 2, (half + 1) * FC // 2):
                        for kc in range(KC):
                            m = pe.matmul(ps[:, 2 + half, (c % 4) * P:(c % 4 + 1) * P], w1[:, kc, c * P:(c + 1) * P], xnT[:, t % BODY, kc, :],
                                          start=(kc == 0), stop=(kc == KC - 1))
                    m.then_inc(S["hidden_ready"], 1)

            def down(t):
                pe.wait_ge(S["gelu_ready"], 2 * t + 1)
                if t == 2:
                    pe.wait_ge(S["c2_taken"], 2)
                if t >= 3:
                    pe.wait_ge(S["y_taken"], t - 2)
                for c in range(FC):
                    if c == FC // 2:
                        pe.wait_ge(S["gelu_ready"], 2 * t + 2)
                    m = pe.matmul(ps[:, 4 + t % 3, 0:D], hT[:, t % 2, c, :], w2[:, c, :], start=(c == 0), stop=(c == FC - 1))
                m.then_inc(S["y_ready"], 1)

            pe.transpose(ps[:, 6, 0:FC], b1r[:, :], ident[0:FC, 0:FC]).then_inc(S["c2_multiplied"], 1)
            turn_tokens(0)
            for t in range(NB + 1):
                if t < NB:
                    up(t)
                    if t + 1 < NB:
                        turn_tokens(t + 1)
                if t:
                    down(t - 1)
                if t == WT_AT:
                    pe.wait_ge(S["weight_ready"], NB)
                    pe.transpose(ps[0:NB, 7, 0:P], wtok[:, :], ident[:, :]).then_inc(S["weights_turned"], 1)

        @block.scalar
        def _(act):
            act.wait_ge(S["constants_ready"], 15)

            def deviation(base, n, mvs):
                act.wait_ge(S["mean_var_ready"], mvs)
                act.activation(sd[:, base:base + n], mv[:, base:base + n, 1:2].rearrange("p a b -> p (a b)"), ACT.Sqrt, bias=eps[:, 0:1]).then_inc(S["deviation_ready"], 1)

            def evacuate_kq(t):
                act.wait_ge(S["kq_projected"], t + 1)
                act.activation(kq[:, :, t * P:(t + 1) * P], ps[:, 4 + t % 2, 0:2 * P].rearrange("p (c n) -> p c n", c=2), ACT.Copy).then_inc(S["kq_taken"], 1)

            deviation(0, BODY, BODY)
            for t in range(NB):
                if t == 1:
                    deviation(BODY, BODY, 2 * BODY)
                if t % BODY == 4 and t + BODY + 1 < NB:
                    deviation(t + 1 + BODY, BODY, t + 1 + 2 * BODY)
                act.wait_ge(S["xn_turned"], t + 1)
                if t >= BODY:
                    act.wait_ge(S["kq_projected"], t - BODY + 1)
                act.activation(xnT[:, t % BODY, :, :], ps[:, t % 2, 0:D].rearrange("p (c n) -> p c n", c=KC), ACT.Copy).then_inc(S["xnT_ready"], 1)
                if t:
                    evacuate_kq(t - 1)
            evacuate_kq(NB - 1)

            def exponentiate(i):
                lo, hi = i * BODY * P, min((i + 1) * BODY * P, N)
                act.activation(kq[:, 0, lo:hi], kq[:, 0, lo:hi], ACT.Exp, bias=kmax[:, 1:2], accum_out=ksums[:, i:i + 1]).then_inc(S["k_exp"], 1)

            act.wait_ge(S["kmax_steps"], 2)
            exponentiate(0)
            exponentiate(1)
            for t in range(NB):
                if t % BODY == 0 and t // BODY + 2 < NB // BODY:
                    exponentiate(t // BODY + 2)
                act.wait_ge(S["ek_turned"], t + 1)
                if t >= BODY:
                    act.wait_ge(S["context_summed"], t - BODY + 1)
                act.activation(ekt[:, t % BODY, :], ps[:, TURN_BANKS[t % 3], 0:P], ACT.Copy).then_inc(S["ek_taken"], 1)

            act.wait_ge(S["ranges_loaded"], 32)
            n, n3, n5, copies, cursor, blocks, joined = registers(act, 4, 3, 5, 5, 0, 1, 1)
            regs = [registers(act, 0, 0, 0) for _ in range(LISTS)]

            def rescale(f, p, b, done, count, fdone):
                act.sem_inc(S["act_go"], 1)
                act.activation(f[:, p:p + 1], Rlast[:, bass.ds(b, 1)], ACT.Exp, bias=negR[:, p:p + 1]).then_inc(S[done], 1)
                act.wait_ge(S[done], count)
                act.sem_inc(S["act_go"], 1)
                act.activation(Rlast[:, bass.ds(b, 1)], Rsb[:, p:p + 1], ACT.Copy).then_inc(S[fdone], 1)

            def split_sums(q):
                first, start, _ = blocks_of(act, regs, q)
                with act.If(first < start):
                    act.wait_ge(S["summed_last"], n)
                    act.sem_inc(S["act_go"], 1)
                    before = act.snap(n, min_val=5, max_val=NG + 4) - 5
                    for half in range(2):
                        act.activation(parts[:, half, :], ps[:, 3 + q % 2, 0:ROW], ACT.Copy, scale=mask[:, half, bass.ds(before, 1)]).then_inc(S["sums_split"], 1)

            def step(g, q):
                p = q % 2
                if q % 2 == 0:
                    load_ranges(act, regs, cursor, q)
                first, start, last = blocks_of(act, regs, q)
                act.wait_ge(S["max_spread"], n)
                act.activation(negR[:, p:p + 1], ps[:, 5, 0:1], ACT.Copy, scale=-1.0).then_inc(S["max_copied"], 1)
                act.activation(Rsb[:, p:p + 1], ps[:, 5, 0:1], ACT.Copy).then_inc(S["max_copied"], 1)
                act.wait_ge(S["summed_last"], n3)
                act.wait_ge(S["max_copied"], copies)
                act.activation(msg[:, p, :, HF:ROW], et[:, p, 0:16].rearrange("p (k h) -> p k h", k=TILES), ACT.Exp, bias=negR[:, p:p + 1]).then_inc(S["exp_ready"], 1)
                act.wait_ge(S["added_last"], n)
                act.wait_ge(S["max_kept_last"], n)
                act.wait_ge(S["max_kept_first"], joined)
                act.sem_inc(S["act_go"], 1)
                if g != 0:
                    split_sums((q - 1) % LISTS)
                with act.If(start < last):
                    with act.Fori(start, last) as b:
                        act.wait_ge(S["added_block"], blocks)
                        act.wait_ge(S["max_kept_block"], blocks)
                        act.reg_add(blocks, blocks, 1)
                        rescale(fsc, p, b, "factor_block", blocks, "max_kept_block")
                with act.If(first < start):
                    act.reg_add(joined, joined, 1)
                    rescale(fscM, p, first, "factor_first", joined, "max_kept_first")
                act.wait_ge(S["added_block"], blocks)
                act.wait_ge(S["max_kept_block"], blocks)
                act.wait_ge(S["max_kept_first"], joined)
                rescale(fsc, p, last, "factor_last", n5, "max_kept_last")
                for r, by in ((n, 1), (n3, 1), (n5, 1), (copies, 2)):
                    act.reg_add(r, r, by)
            act.wait_ge(S["masks_ready"], 2)
            groups(step)(act)
            act.wait_ge(S["added_last"], n)
            split_sums((NG - 1) % LISTS)
            act.wait_ge(S["max_kept_last"], n)
            act.wait_ge(S["max_kept_block"], blocks)
            act.wait_ge(S["max_kept_first"], joined)
            act.activation(Fin[:, :], Rlast[:, :], ACT.Exp, bias=negR[:, (NG - 1) % 2:(NG - 1) % 2 + 1]).then_inc(S["final_factors"], 1)

            act.wait_ge(S["c2_multiplied"], 2)
            act.activation(b1[:, :], ps[:, 6, 0:FC], ACT.Copy).then_inc(S["c2_taken"], 1)

            def take_tokens(t):
                act.wait_ge(S["xn2_turned"], t + 1)
                if t >= BODY:
                    act.wait_ge(S["hidden_ready"], 2 * (t - BODY + 1))
                act.activation(xnT[:, t % BODY, :, :], ps[:, t % 2, 0:D].rearrange("p (c n) -> p c n", c=KC), ACT.Copy).then_inc(S["xn2T_ready"], 1)

            for base, n in FIRST_BATCHES:
                deviation(base, n, NB + base + n)
                if base == 0:
                    take_tokens(0)
            act.activation(negR[:, 0:1], eps[:, 0:1], ACT.Gelu_apprx_tanh).then_inc(S["gelu_table"], 1)
            for t in range(NB):
                if t + 1 < NB:
                    take_tokens(t + 1)
                if t >= 2:
                    act.wait_ge(S["y_ready"], t - 1)
                for half in range(2):
                    act.wait_ge(S["hidden_ready"], 2 * t + 1 + half)
                    for c in range(half * FC // 2, (half + 1) * FC // 2):
                        m = act.activation(hT[:, t % 2, c, :], ps[:, 2 + half, (c % 4) * P:(c % 4 + 1) * P], ACT.Gelu_apprx_tanh, bias=b1[:, c:c + 1])
                    m.then_inc(S["gelu_ready"], 1)
                if t == BODY - 2:
                    deviation(BODY, NB - BODY, 2 * NB)
                if t == WT_AT:
                    act.wait_ge(S["weights_turned"], 1)
                    act.activation(wtT[:, :], ps[0:NB, 7, 0:P], ACT.Copy).then_inc(S["weights_taken"], 1)

        @block.vector
        def _(dve):
            dve.wait_ge(S["constants_ready"], 14)
            dve.tensor_scalar(ident[:, :], iota[:, :], part[:, 0:1], None, ALU.is_equal).then_inc(S["constants_ready"], 1)
            dve.tensor_scalar(tri[:, :], iota[:, :], part[:, 0:1], None, ALU.is_lt)

            def statistics(base, n, st0):
                for j in range(n):
                    dve.bn_stats(stats[:, j, :], x[:, base + j, :]).then_inc(S["stats_ready"], 1)
                dve.wait_ge(S["stats_ready"], st0 + n)
                for j in range(n):
                    dve.bn_aggr(mv[:, base + j, :], stats[:, j, :]).then_inc(S["mean_var_ready"], 1)

            def invert(base, n, k):
                dve.wait_ge(S["deviation_ready"], k)
                dve.reciprocal(rstd[:, base:base + n], sd[:, base:base + n]).then_inc(S["rstd_ready"], 1)
                dve.wait_ge(S["rstd_ready"], k)

            def normed(t):
                return dve.tensor_scalar(xn[:, t % BODY, :], x[:, t, :], mv[:, t, 0:1], rstd[:, t:t + 1], ALU.subtract, ALU.mult)

            def evacuate_h(t):
                dve.wait_ge(S["h_projected"], t + 1)
                if t >= BODY:
                    dve.wait_ge(s_tab[t % BODY], 16 * (t // BODY))
                dve.tensor_copy(hst[:, t % BODY, :], ps[:, 2 + t % 2, 0:ROW]).then_inc(S["rows_staged"], 1)
                dve.tensor_copy(adv[:, t, :], ps[:, 2 + t % 2, ROW:HW]).then_inc(S["attn_dst_v_taken"], 1)

            dve.wait_ge(s_x[0], 16)
            statistics(0, BODY, 0)
            dve.wait_ge(S["a_loaded"], 32)
            dve.wait_ge(S["w_loaded"], 32)
            for s in range(2):
                dve.tensor_tensor(aprod[:, s, :, :], wbig[:, :, 0:HF], avec[:, s:s + 1, :].to_broadcast([P, KC, HF]), ALU.mult).then_inc(S["w_times_a"], 1)
            dve.wait_ge(S["w_times_a"], 2)
            for s in range(2):
                m = dve.tensor_reduce(wbig[:, :, HF + s * HEADS:HF + (s + 1) * HEADS], aprod[:, s, :, :].rearrange("p c (h o) -> p c h o", h=HEADS), AX.X, ALU.add)
            m.then_inc(S["w_a_ready"], 1)
            invert(0, BODY, 1)
            for t in range(BODY):
                normed(t).then_inc(S["xn_ready"], 1)

            def one_block_statistics(t):
                if t % BODY == 0:
                    dve.wait_ge(s_x[t // BODY], 16 if t < NB - BODY else 32)
                    dve.wait_ge(S["mean_var_ready"], t)
                dve.bn_stats(stats[:, t % BODY, :], x[:, t, :]).then_inc(S["stats_ready"], 1)
                if t % BODY == BODY - 1:
                    dve.wait_ge(S["stats_ready"], t + 1)
                    for j in range(BODY):
                        dve.bn_aggr(mv[:, t + 1 - BODY + j, :], stats[:, j, :]).then_inc(S["mean_var_ready"], 1)

            for t in range(BODY, 2 * BODY):
                one_block_statistics(t)
            invert(BODY, BODY, 2)
            for t in range(NB):
                i, j = t // BODY, t % BODY
                if i + 2 < NB // BODY:
                    for k in ((0, 1), (2,), (3,), (4,), ())[j]:
                        one_block_statistics((i + 2) * BODY + k)
                    if j == BODY - 1:
                        invert((i + 2) * BODY, BODY, i + 3)
                if t == 0:
                    dve.wait_ge(S["dst_loaded"], 48)
                    dve.tensor_copy(du[:, :], dl[:, :]).then_inc(S["table_steps"], 1)
                    dve.wait_ge(S["table_steps"], 1)
                    dve.tensor_scalar(dm, dl[:, :], P - 1, None, ALU.bitwise_and).then_inc(S["table_steps"], 1)
                    dve.wait_ge(S["table_steps"], 2)
                    dve.tensor_reduce(dn[:, 0:1], dl[:, :], AX.X, ALU.min).then_inc(S["table_steps"], 1)
                    dve.wait_ge(S["table_steps"], 3)
                    dve.tensor_reduce(dn[:, 1:2], dl[:, :], AX.X, ALU.max).then_inc(S["table_steps"], 1)
                    dve.wait_ge(S["table_steps"], 4)
                    dve.tensor_scalar(mm[:, 0:1], dn[:, 0:1], 7, None, ALU.arith_shift_right).then_inc(S["table_steps"], 1)
                    dve.wait_ge(S["table_steps"], 5)
                    dve.tensor_scalar(mm[:, 2:3], dn[:, 1:2], 7, None, ALU.arith_shift_right).then_inc(S["table_steps"], 1)
                    dve.wait_ge(S["table_steps"], 6)
                    dve.tensor_scalar(dn[:, 6:7], dn[:, 0:1], P - 1, None, ALU.bitwise_and).then_inc(S["table_steps"], 1)
                    dve.wait_ge(S["table_steps"], 7)
                    dve.tensor_tensor(dn[:, 2:3], dn[:, 1:2], dn[:, 0:1], ALU.subtract).then_inc(S["table_steps"], 1)
                    dve.wait_ge(S["table_steps"], 8)
                    dve.tensor_tensor(dn[:, 3:4], mm[:, 2:3], mm[:, 0:1], ALU.subtract).then_inc(S["table_steps"], 1)
                    dve.wait_ge(S["table_steps"], 9)
                    dve.tensor_scalar(dn[:, 4:5], dn[:, 2:3], float(P - 1), None, ALU.is_gt).then_inc(S["table_steps"], 1)
                    dve.wait_ge(S["table_steps"], 10)
                    dve.tensor_tensor(dn[:, 5:6], dn[:, 4:5], dn[:, 3:4], ALU.mult).then_inc(S["table_steps"], 1)
                    dve.wait_ge(S["table_steps"], 11)
                    dve.tensor_tensor(mm[:, 1:2], mm[:, 2:3], dn[:, 5:6], ALU.subtract).then_inc(S["table_steps"], 1)
                evacuate_h(t)
                if t + BODY < NB:
                    dve.wait_ge(S["xn_turned"], t + 1)
                    normed(t + BODY).then_inc(S["xn_ready"], 1)
                if j == BODY - 1:
                    dve.wait_ge(S["kq_taken"], t + 1)
                    dve.tensor_reduce(kmaxs[:, i:i + 1], kq[:, 0, i * BODY * P:min((t + 1) * P, N)], AX.X, ALU.max).then_inc(S["kmax_of_batch"], 1)

            dve.wait_ge(S["kmax_of_batch"], NB // BODY)
            dve.tensor_reduce(kmax[:, 0:1], kmaxs[:, :], AX.X, ALU.max).then_inc(S["kmax_steps"], 1)
            dve.wait_ge(S["kmax_steps"], 1)
            dve.tensor_scalar(kmax[:, 1:2], kmax[:, 0:1], -1.0, None, ALU.mult).then_inc(S["kmax_steps"], 1)
            dve.memset(kq[:, 0, N:NB * P], 0.0).then_inc(S["k_padding_zero"], 1)

            dve.wait_ge(S["attn_dst_v_taken"], NB)
            dve.tensor_copy(ad3[:, :, 0, :], adv[:, :, 0:HEADS]).then_inc(S["split_steps"], 1)
            dve.wait_ge(S["split_steps"], 1)
            dve.tensor_tensor(adr[:, :, 0, :], adv[:, :, 0:HEADS], ad3[:, :, 0, :], ALU.subtract).then_inc(S["split_steps"], 1)
            dve.wait_ge(S["split_steps"], 2)
            dve.tensor_copy(ad3[:, :, 1, :], adr[:, :, 0, :]).then_inc(S["split_steps"], 1)
            dve.wait_ge(S["split_steps"], 3)
            dve.tensor_tensor(adr[:, :, 1, :], adr[:, :, 0, :], ad3[:, :, 1, :], ALU.subtract).then_inc(S["split_steps"], 1)
            dve.wait_ge(S["split_steps"], 4)
            dve.tensor_copy(ad3[:, :, 2, :], adr[:, :, 1, :]).then_inc(S["attn_dst_split"], 1)

            dve.wait_ge(S["ranges_loaded"], 32)
            dve.wait_ge(S["acc_zeroed"], 1)
            dve.tensor_scalar(mask[:, 0, :], low[:, :], part[:, 0:1], None, ALU.is_le).then_inc(S["masks_ready"], 1)
            dve.tensor_scalar(mask[:, 1, :], low[:, :], part[:, 0:1], None, ALU.is_gt).then_inc(S["masks_ready"], 1)
            n, cursor, lists, rows, marked, visited, after, joined, parts_made = registers(dve, 4, 0, 0, 0, 1, 1, 0, 1, 2)
            regs = [registers(dve, 0, 0, 0) for _ in range(LISTS)]

            def columns(q, ready, weight=lambda: None, reduce=lambda: None):
                def of_last():
                    dve.tensor_scalar(ohT[:, 0, :], dstb[:, q, :], nodeid[:, bass.ds(last, 1)], None, ALU.is_equal).then_inc(S["columns_last"], 1)

                first, _, last = blocks_of(dve, regs, q)
                dve.wait_ge(s_list[q], lists)
                dve.wait_ge(S["attn_dst_last"], ready)
                dve.sem_inc(S["dve_go"], 1)
                with dve.If(first < last):
                    weight()
                    reduce()
                    with dve.Fori(first, last) as b:
                        dve.wait_ge(S["attn_dst_block"], marked)
                        dve.sem_inc(S["dve_go"], 1)
                        dve.tensor_scalar(ohT[:, 1, :], dstb[:, q, :], nodeid[:, bass.ds(b, 1)], None, ALU.is_equal).then_inc(S["columns_block"], 1)
                        dve.reg_add(marked, marked, 1)
                    of_last()
                with dve.Else():
                    weight()
                    of_last()
                    reduce()

            def look_up(q):
                if q % 2 == 0:
                    load_ranges(dve, regs, cursor, q)
                if q == 0:
                    dve.reg_add(lists, lists, 16 * 5)

            def logits(q, ready, g=None):
                p = q % 2
                e = et[:, p, 0:16]
                e16 = e.rearrange("p (k h) -> p k h", k=TILES)

                def add():
                    if q % RING == 0:
                        dve.reg_add(rows, rows, 16 * TILES)
                    dve.wait_ge(s_g[q % RING], rows)
                    if g == NG - 1:
                        dve.wait_ge(S["padding_loaded"], 48)
                    dve.wait_ge(S["attn_dst_last"], ready)
                    dve.tensor_tensor(e16, ps[:, p, 0:16].rearrange("p (k h) -> p k h", k=TILES), G[:, q % RING, :, HF:ROW], ALU.add).then_inc(S["logit_sum"], 1)

                def leak():
                    dve.wait_ge(S["logit_sum"], ready)
                    dve.scalar_tensor_tensor(out=e, in0=e, scalar=NEG_SLOPE, in1=e, op0=ALU.mult, op1=ALU.max).then_inc(S["logit_leaky"], 1)

                def weight():
                    dve.wait_ge(S["logit_leaky"], ready)
                    dve.tensor_tensor(e16, e16, wtr[:, q, :].unsqueeze(2).to_broadcast([P, TILES, HEADS]), ALU.mult).then_inc(S["logit_weighted"], 1)

                def reduce():
                    dve.wait_ge(S["logit_weighted"], ready)
                    dve.tensor_reduce(rm[:, p:p + 1], e, AX.X, ALU.max).then_inc(S["edge_max"], 1)
                return add, leak, weight, reduce

            def group_max(q, ready):
                dve.wait_ge(S["max_turned"], ready)
                before = LOWEST if ready == 3 else rg[:, (q + 1) % 2:(q + 1) % 2 + 1]
                dve.tensor_scalar(rj[:, :], ps[0:1, 2, 0:P], before, LOWEST, ALU.max, ALU.max, accum_out=rg[:, q % 2:q % 2 + 1]).then_inc(S["running_max"], 1)

            def messages(q):
                p = q % 2
                dve.wait_ge(S["exp_ready"], n)
                ex = msg[:, p, :, HF:ROW].unsqueeze(3).to_broadcast([P, TILES, HEADS, OUT_F])
                dve.tensor_tensor(msg[:, p, :, 0:HF].rearrange("p k (h o) -> p k h o", h=HEADS),
                                  G[:, q % RING, :, 0:HF].rearrange("p k (h o) -> p k h o", h=HEADS), ex, ALU.mult).then_inc(S["messages_ready"], 1)

            def add_block(b, factor, sums, done):
                a = acc[:, bass.ds(b, 1), :].rearrange("p a c -> p (a c)")
                dve.scalar_tensor_tensor(out=a, in0=a, scalar=factor, in1=sums, op0=ALU.mult, op1=ALU.add).then_inc(S[done], 1)

            def one_hot(g, q, b, done):
                d = dlast[:, :] if g == NG - 1 else dcr[:, q, :]
                dve.tensor_tensor(oh[:, q % 2, :, :], iotab[:, bass.ds(b, 1), :].to_broadcast([P, TILES, P]), d.unsqueeze(2).to_broadcast([P, TILES, P]), ALU.is_equal).then_inc(S[done], 1)

            def add_last(q, between=lambda: None):
                first, start, last = blocks_of(dve, regs, q)
                p = q % 2
                total = ps[:, 3 + p, 0:ROW]
                dve.wait_ge(S["summed_last"], n)
                dve.wait_ge(S["factor_last"], n)
                dve.wait_ge(S["added_last"], n)
                dve.wait_ge(S["added_block"], visited)
                dve.sem_inc(S["dve_go"], 1)
                with dve.If(first < start):
                    dve.reg_add(joined, joined, 1)
                    dve.reg_add(parts_made, parts_made, 2)
                    dve.wait_ge(S["factor_first"], joined)
                    dve.wait_ge(S["sums_split"], parts_made)
                    dve.sem_inc(S["dve_go"], 1)
                    add_block(first, fscM[:, p:p + 1], parts[:, 0, :], "added_first")
                    between()
                    dve.wait_ge(S["added_first"], joined)
                    dve.sem_inc(S["dve_go"], 1)
                    add_block(last, fsc[:, p:p + 1], parts[:, 1, :], "added_last")
                with dve.Else():
                    add_block(last, fsc[:, p:p + 1], total, "added_last")
                    between()

            def visit(g, q, between):
                _, start, last = blocks_of(dve, regs, q)
                with dve.If(start < last):
                    if g != 0:
                        add_last((q - 1) % LISTS)
                    dve.reg_add(after, n, 1)
                    if g != 0:
                        dve.wait_ge(S["added_last"], after)
                        dve.sem_inc(S["dve_go"], 1)
                    with dve.Fori(start, last) as b:
                        one_hot(g, q, b, "onehot_block")
                        dve.wait_ge(S["added_block"], visited)
                        dve.reg_add(visited, visited, 1)
                        dve.wait_ge(S["summed_block"], visited)
                        dve.wait_ge(S["factor_block"], visited)
                        dve.sem_inc(S["dve_go"], 1)
                        add_block(b, fsc[:, q % 2:q % 2 + 1], ps[:, 3 + q % 2, 0:ROW], "added_block")
                    one_hot(g, q, last, "onehot_last")
                    if g is None or g + 1 < NG:
                        group_max(q + 1, n)
                    between()
                with dve.Else():
                    dve.tensor_tensor(oh[:, q % 2, :, :], iota[:, :].unsqueeze(1).to_broadcast([P, TILES, P]),
                                      dmr[:, q, :].unsqueeze(2).to_broadcast([P, TILES, P]), ALU.is_equal).then_inc(S["onehot_last"], 1)
                    if g is None or g + 1 < NG:
                        group_max(q + 1, n)
                    if g != 0:
                        add_last((q - 1) % LISTS, between)
                    else:
                        between()

            look_up(0)
            look_up(2)
            columns(0, 1)
            columns(1, 2)
            for operation in logits(0, 2):
                operation()
            group_max(0, 3)
            for operation in logits(1, 3):
                operation()
            columns(2, 3)

            dve.wait_ge(S["k_exp"], NB // BODY)
            dve.tensor_reduce(ksum[:, 0:1], ksums[:, :], AX.X, ALU.add).then_inc(S["ksum_steps"], 1)
            dve.wait_ge(S["ksum_steps"], 1)
            dve.reciprocal(ksum[:, 1:2], ksum[:, 0:1]).then_inc(S["ksum_steps"], 1)
            dve.wait_ge(S["context_summed"], NB)
            for h in range(MIX_HEADS):
                s = slice(h * DIM_HEAD, (h + 1) * DIM_HEAD)
                dve.tensor_copy(ctxT[s, s], ps[s, 7, s]).then_inc(S["context_taken"], 1)
            dve.wait_ge(S["c2_multiplied"], 1)
            dve.wait_ge(S["ksum_steps"], 2)
            dve.tensor_scalar(C2[:, :], ps[:, 6, 0:D], ksum[:, 1:2], float(DIM_HEAD) ** -0.5, ALU.mult, ALU.mult).then_inc(S["c2_taken"], 1)
            dve.wait_ge(S["b_out_added"], NB)
            for t in range(NB):
                dve.wait_ge(S["mix_multiplied"], t + 1)
                dve.tensor_tensor(x[:, t, :], ps[:, MIX_BANKS[t % 4], 0:D], x[:, t, :], ALU.add).then_inc(S["mix_added"], 1)

            def step(g, q):
                add, leak, weight, reduce = [lambda: None] * 4
                if g is None or g + 2 < NG:
                    add, leak, weight, reduce = logits((q + 2) % LISTS, n, g if g is None else g + 2)
                messages(q)
                if g is None or g + 3 < NG:
                    look_up((q + 3) % LISTS)
                visit(g, q, add)
                leak()
                if g is None or g + 3 < NG:
                    columns((q + 3) % LISTS, n, weight, reduce)
                else:
                    weight()
                    reduce()
                dve.reg_add(n, n, 1)
            dve.wait_ge(S["block_iota_ready"], 1)
            dve.wait_ge(S["last_dst_loaded"], 16)
            groups(step)(dve)
            add_last((NG - 1) % LISTS)
            dve.reg_add(n, n, 1)
            dve.wait_ge(S["added_last"], n)
            dve.wait_ge(S["added_block"], visited)

            dve.wait_ge(S["final_factors"], 1)
            fb = Fin[:, :].unsqueeze(2).to_broadcast([P, NB, HEADS])
            dve.tensor_tensor(rden[:, 0, :, :], acc[:, 0:NB, HF:ROW], fb, ALU.mult).then_inc(S["denominator_steps"], 1)
            dve.wait_ge(S["denominator_steps"], 1)
            dve.tensor_scalar(rden[:, 1, :, :], rden[:, 0, :, :], DEN_EPS, None, ALU.add).then_inc(S["denominator_steps"], 1)
            dve.wait_ge(S["denominator_steps"], 2)
            dve.reciprocal(rden[:, 0, :, :], rden[:, 1, :, :]).then_inc(S["denominator_steps"], 1)
            dve.wait_ge(S["denominator_steps"], 3)
            dve.tensor_tensor(rden[:, 1, :, :], rden[:, 0, :, :], fb, ALU.mult).then_inc(S["denominator_steps"], 1)
            dve.wait_ge(S["denominator_steps"], 4)

            def add_graph(base, n):
                for j in range(n):
                    t = base + j
                    r = rden[:, 1, t, :].unsqueeze(2).to_broadcast([P, HEADS, OUT_F])
                    dve.tensor_tensor(gsc[:, j, :].rearrange("p (h o) -> p h o", h=HEADS), acc[:, t, 0:HF].rearrange("p (h o) -> p h o", h=HEADS), r, ALU.mult).then_inc(S["x1_steps"], 1)
                dve.wait_ge(S["x1_steps"], 2 * base + n)
                for j in range(n):
                    t = base + j
                    dve.tensor_tensor(x[:, t, :], x[:, t, :], gsc[:, j, :], ALU.add).then_inc(S["x1_steps"], 1)
                dve.wait_ge(S["x1_steps"], 2 * (base + n))
                statistics(base, n, NB + base)

            def norm_tokens(t):
                dve.tensor_scalar(acc[:, t, 0:D], x[:, t, :], mv[:, t, 0:1], rstd[:, t:t + 1], ALU.subtract, ALU.mult).then_inc(S["xn2_ready"], 1)

            def weigh_tokens(t):
                dve.wait_ge(S["xn2_ready"], t + 1)
                if t:
                    dve.wait_ge(S["weight_ready"], t)
                dve.tensor_tensor_reduce(wprod[:, :], acc[:, t, 0:D], wrb[:, :], 1.0, brb[:, 0:1], ALU.mult, ALU.add, wtok[:, t:t + 1]).then_inc(S["weight_ready"], 1)

            def take_output(t):
                dve.wait_ge(S["y_ready"], t + 1)
                dve.wait_ge(S["xn2_added"], t + 1)
                dve.wait_ge(S["weight_ready"], t + 1)
                dve.tensor_tensor(acc[:, t, 0:D], ps[:, 4 + t % 3, 0:D], b2b[:, :], ALU.add).then_inc(S["y_taken"], 1)

            for k, (base, n) in enumerate(FIRST_BATCHES):
                add_graph(base, n)
                invert(base, n, NB // BODY + 1 + k)
                for t in range(base, base + n):
                    norm_tokens(t)
            for i in range(1, NB // BODY):
                add_graph(i * BODY, BODY)
            invert(BODY, NB - BODY, NB // BODY + 1 + len(FIRST_BATCHES))
            for t in range(BODY, NB):
                norm_tokens(t)
                weigh_tokens(t - BODY)
                if t % 4 == 3:
                    take_output(t // 4 - 1)
            for t in range(NB - BODY, NB):
                weigh_tokens(t)
            taken = NB // 4 - 1

            def rank_tokens(t):
                wt = wtok[:, t:t + 1]
                lo, hi = t * P, min((t + 1) * P, N)
                if t:
                    dve.wait_ge(S["counted"], 3 * t)
                    dve.tensor_scalar(junk[:, 0:lo], wrow[:, 0:lo], wt, 0.0, ALU.is_ge, ALU.add, accum_out=cnt[:, t, 0:1]).then_inc(S["counted"], 1)
                else:
                    dve.memset(cnt[:, t, 0:1], 0.0).then_inc(S["counted"], 1)
                dve.tensor_scalar(junk[:, lo:N], wrow[:, lo:N], wt, 0.0, ALU.is_gt, ALU.add, accum_out=cnt[:, t, 1:2]).then_inc(S["counted"], 1)
                dve.scalar_tensor_tensor(out=wprod[:, 0:hi - lo], in0=wrow[:, lo:hi], scalar=wt, in1=tri[:, 0:hi - lo], op0=ALU.is_equal, op1=ALU.mult, accum_out=cnt[:, t, 2:3]).then_inc(S["counted"], 1)
                dve.wait_ge(S["counted"], 3 * t + 3)
                dve.tensor_reduce(rank[:, t:t + 1], cnt[:, t, :], AX.X, ALU.add).then_inc(S["rank_steps"], 1)
                dve.wait_ge(S["rank_steps"], 2 * t + 1)
                dve.scalar_tensor_tensor(out=mw[:, t:t + 1], in0=rank[:, t:t + 1], scalar=float(KK), in1=wt, op0=ALU.is_lt, op1=ALU.mult).then_inc(S["rank_steps"], 1)

            ranked = 0
            for t in range(taken, NB):
                take_output(t)
                if t == WT_AT + 1:
                    dve.wait_ge(S["weights_spread"], 16)
                if t >= WT_AT + 1:
                    for _ in range(min(1 + t % 2, NB - ranked)):
                        rank_tokens(ranked)
                        ranked += 1
            assert ranked == NB


_INS = ["x", "src", "dst", "edge_weight", "L0_gnn_W", "L0_gnn_a_src", "L0_gnn_a_dst", "L0_mix_W_qkv", "L0_mix_W_out",
        "L0_mix_b_out", "L0_ffn_wr", "L0_ffn_br", "L0_ffn_w1", "L0_ffn_b1", "L0_ffn_w2", "L0_ffn_b2"]


def kernel(**inputs):
    import concourse.bacc as _bacc
    from concourse.bass_utils import run_bass_kernel_spmd as _run

    nc = _bacc.Bacc("TRN2", target_bir_lowering=False, num_devices=1)
    arrays, args = {}, []
    for name in _INS:
        a = np.ascontiguousarray(inputs[name])
        arrays[f"in_{name}"] = a
        args.append(nc.dram_tensor(f"in_{name}", a.shape, mybir.dt.from_np(a.dtype), kind="ExternalInput").ap())
    out = nc.dram_tensor("out_0", inputs["x"].shape, F32, kind="ExternalOutput").ap()
    gps_layer(nc, *args, out)
    r = _run(nc, [arrays], core_ids=[0])
    return r.results[0]["out_0"]
```
